# Optimizing a Trainium2 kernel written in Bass

```python
import numpy as np
import jax
import jax.numpy as jnp

def _softmax(x, axis=-1):
    return jax.nn.softmax(x, axis=axis)

def _gelu(x):
    return jax.nn.gelu(x, approximate=True)

def _silu(x):
    return jax.nn.silu(x)

def _sigmoid(x):
    return jax.nn.sigmoid(x)

def _layernorm(x, axis=-1, eps=1e-05):
    m = jnp.mean(x, axis=axis, keepdims=True)
    v = jnp.var(x, axis=axis, keepdims=True)
    return (x - m) / jnp.sqrt(v + eps)

def _scatter_add(tgt, idx, src, axis=0):
    return tgt.at[idx].add(src)

def _segment_sum(src, seg, n):
    return jax.ops.segment_sum(src, seg, n)
kernel_name = 'mk_xattn_ffn_d1_seqx_r4_82780e'

def setup_inputs(seed: int=0):
    np.random.seed(seed)
    _w = jnp.asarray

    def _rec_inputs():
        import jax
        import jax.numpy as jnp
        _rk = jax.random.key(seed)
        x = -0.0005207 + 1.001 * jax.random.normal(jax.random.fold_in(_rk, 1), (4, 1024, 256), jnp.float32)
        _lenS = 1024 - jax.random.randint(jax.random.fold_in(_rk, 7), (4,), 0, max(1, 1024 // 4) + 1, jnp.int32)
        _lenS2 = 77 - jax.random.randint(jax.random.fold_in(_rk, 8), (4,), 0, max(1, 77 // 4) + 1, jnp.int32)
        _ctx_1024P = jax.random.normal(jax.random.fold_in(_rk, 12), (4, 16, 256), jnp.float32)
        _ctx_1024c = jax.random.dirichlet(jax.random.fold_in(_rk, 512), 0.3 * jnp.ones((16,), jnp.float32), (4, 77))
        _ctx_1024t = jnp.einsum('bsk,bkd->bsd', _ctx_1024c, _ctx_1024P)
        _ctx_1024t = _ctx_1024t * jax.lax.rsqrt(jnp.mean(jnp.square(_ctx_1024t)) + 1e-12) * 0.953939
        ctx_1024 = 0.00191187 + 0.999416 * (_ctx_1024t + 0.3 * jax.random.normal(jax.random.fold_in(_rk, 612), (4, 77, 256), jnp.float32))
        _validS = jnp.arange(1024)[None, :] < _lenS[:, None]
        _validS2 = jnp.arange(77)[None, :] < _lenS2[:, None]
        _causal = jnp.tril(jnp.ones((1024, 1024), dtype=bool))
        mask_BxS_ff1 = jnp.where(jnp.ones((4, 1024), dtype=bool), 1.0, 0.0).astype(jnp.float32)
        mask_BxS2_ik0 = jnp.where(jnp.broadcast_to(_validS2[:, :], (4, 77)), 0, 1).astype(jnp.int32)
        return (x, ctx_1024, mask_BxS_ff1, mask_BxS2_ik0)
    x, ctx_1024, mask_BxS_ff1, mask_BxS2_ik0 = _rec_inputs()

    def _L0_xattn_setup():
        import jax, jax.numpy as jnp
        import numpy as np
        B, F, T, D = (8, 64, 32, 256)
        NEG = -1e+30
        key = jax.random.key(seed)
        ks = jax.random.split(key, 10)
        s = 1.0 / np.sqrt(D)
        return {'features': jax.random.normal(ks[0], (B, F, D), jnp.float32), 'masks': jnp.ones((B, F), jnp.float32), 'textual_features': jax.random.normal(ks[1], (B, T, D), jnp.float32), 'q_masks': jax.random.randint(ks[2], (B, T), 0, 2, jnp.int32), 'Ws': jax.random.normal(ks[3], (D, D), jnp.float32) * s, 'W': jax.random.normal(ks[4], (D, D), jnp.float32) * s, 'w': jax.random.normal(ks[5], (D, 1), jnp.float32) * s, 'b': jax.random.normal(ks[6], (1, D), jnp.float32) * s, 'Wcw': jax.random.normal(ks[7], (1, D), jnp.float32) * s, 'bcw': jnp.zeros((1,), jnp.float32), 'Wcb': jax.random.normal(ks[8], (1, D), jnp.float32) * s, 'bcb': jnp.zeros((1,), jnp.float32)}
    _L0_xattn_all = _L0_xattn_setup()
    _L0_xattn_in = {k: v for k, v in _L0_xattn_all.items() if k in ('Ws', 'W', 'w', 'b', 'Wcw', 'bcw', 'Wcb', 'bcb')}
    del _L0_xattn_all

    def _L0_ffn_setup():
        import jax, jax.numpy as jnp
        import numpy as np
        NUM_EXPERTS = 8
        CAP_FACTOR = 1.0
        MIN_CAP = 8
        key = jax.random.key(seed)
        ks = jax.random.split(key, 10)
        G, S, D, H, E = (4, 1024, 256, 1024, NUM_EXPERTS)
        s = 0.02
        return {'x': jax.random.normal(ks[0], (G, S, D), dtype=jnp.float32), 'gate': jax.random.normal(ks[1], (D, E), dtype=jnp.float32) * s, 'W1': jax.random.normal(ks[2], (E, D, H), dtype=jnp.float32) * s, 'b1': jnp.zeros((E, H), dtype=jnp.float32), 'W2': jax.random.normal(ks[3], (E, H, D), dtype=jnp.float32) * s, 'b2': jnp.zeros((E, D), dtype=jnp.float32), 'Ws1': jax.random.normal(ks[4], (D, H), dtype=jnp.float32) * s, 'bs1': jnp.zeros((H,), dtype=jnp.float32), 'Ws2': jax.random.normal(ks[5], (H, D), dtype=jnp.float32) * s, 'bs2': jnp.zeros((D,), dtype=jnp.float32)}
    _L0_ffn_all = _L0_ffn_setup()
    _L0_ffn_in = {k: v for k, v in _L0_ffn_all.items() if k in ('gate', 'W1', 'b1', 'W2', 'b2', 'Ws1', 'bs1', 'Ws2', 'bs2')}
    del _L0_ffn_all
    return {'x': x, 'ctx_1024': ctx_1024, 'mask_BxS_ff1': mask_BxS_ff1, 'mask_BxS2_ik0': mask_BxS2_ik0, 'L0_xattn_Ws': _L0_xattn_in['Ws'], 'L0_xattn_W': _L0_xattn_in['W'], 'L0_xattn_w': _L0_xattn_in['w'], 'L0_xattn_b': _L0_xattn_in['b'], 'L0_xattn_Wcw': _L0_xattn_in['Wcw'], 'L0_xattn_bcw': _L0_xattn_in['bcw'], 'L0_xattn_Wcb': _L0_xattn_in['Wcb'], 'L0_xattn_bcb': _L0_xattn_in['bcb'], 'L0_ffn_gate': _L0_ffn_in['gate'], 'L0_ffn_W1': _L0_ffn_in['W1'], 'L0_ffn_b1': _L0_ffn_in['b1'], 'L0_ffn_W2': _L0_ffn_in['W2'], 'L0_ffn_b2': _L0_ffn_in['b2'], 'L0_ffn_Ws1': _L0_ffn_in['Ws1'], 'L0_ffn_bs1': _L0_ffn_in['bs1'], 'L0_ffn_Ws2': _L0_ffn_in['Ws2'], 'L0_ffn_bs2': _L0_ffn_in['bs2']}

def reference(x, ctx_1024, mask_BxS_ff1, mask_BxS2_ik0, L0_xattn_Ws, L0_xattn_W, L0_xattn_w, L0_xattn_b, L0_xattn_Wcw, L0_xattn_bcw, L0_xattn_Wcb, L0_xattn_bcb, L0_ffn_gate, L0_ffn_W1, L0_ffn_b1, L0_ffn_W2, L0_ffn_b2, L0_ffn_Ws1, L0_ffn_bs1, L0_ffn_Ws2, L0_ffn_bs2):
    import jax
    import jax.numpy as jnp

    def _L0_xattn_ref(features, masks, textual_features, q_masks, Ws, W, w, b, Wcw, bcw, Wcb, bcb):
        import jax, jax.numpy as jnp
        import numpy as np
        B, F, T, D = (8, 64, 32, 256)
        NEG = -1e+30
        txt_proj = jnp.einsum('btd,de->bte', textual_features, Ws)
        feat_proj = jnp.einsum('bfd,de->bfe', features, W)
        h = jnp.tanh(txt_proj[:, None, :, :] + feat_proj[:, :, None, :] + b[None, None, :, :][..., 0, :])
        rho = jnp.einsum('bftd,d->bft', h, w[:, 0])
        qm = q_masks.astype(jnp.float32)
        rho = rho + (1.0 - qm)[:, None, :] * NEG
        att = jax.nn.softmax(rho, axis=-1)
        txt_h = jnp.einsum('bft,btd->bfd', att, textual_features)
        w_s = jnp.tanh(jnp.einsum('bfd,od->bfo', txt_h, Wcw) + bcw)
        b_s = jnp.tanh(jnp.einsum('bfd,od->bfo', txt_h, Wcb) + bcb)
        return w_s * features + b_s

    def _L0_ffn_ref(x, gate, W1, b1, W2, b2, Ws1, bs1, Ws2, bs2):
        import jax, jax.numpy as jnp
        import numpy as np
        NUM_EXPERTS = 8
        CAP_FACTOR = 1.0
        MIN_CAP = 8
        G, S, D = x.shape
        E = gate.shape[1]
        T = G * S
        capacity = max(MIN_CAP, int(CAP_FACTOR * T / E))
        logits = jnp.einsum('gsd,de->gse', x, gate)
        probs = jax.nn.softmax(logits, axis=-1)
        flat_probs = probs.transpose(2, 0, 1).reshape(E, T)
        scores, token_idx = jax.lax.top_k(flat_probs, k=capacity)
        scores = jnp.where(scores > -100000000.0, scores, 0.0)
        flat_x = x.reshape(T, D)
        tok = flat_x[token_idx]
        h = jax.nn.gelu(jnp.einsum('ecd,edh->ech', tok, W1) + b1[:, None, :])
        out_tok = jnp.einsum('ech,ehd->ecd', h, W2) + b2[:, None, :]
        scaled = out_tok * scores[..., None]
        routed = jnp.zeros_like(flat_x).at[token_idx.reshape(-1)].add(scaled.reshape(E * capacity, D)).reshape(G, S, D)
        shared = jax.nn.gelu(jnp.einsum('gsd,dh->gsh', x, Ws1) + bs1)
        shared = jnp.einsum('gsh,hd->gsd', shared, Ws2) + bs2
        return routed + shared
    x = x + _L0_xattn_ref(_layernorm(x, axis=-1), mask_BxS_ff1, ctx_1024, mask_BxS2_ik0, L0_xattn_Ws, L0_xattn_W, L0_xattn_w, L0_xattn_b, L0_xattn_Wcw, L0_xattn_bcw, L0_xattn_Wcb, L0_xattn_bcb)
    x = x + _L0_ffn_ref(_layernorm(x, axis=-1), L0_ffn_gate, L0_ffn_W1, L0_ffn_b1, L0_ffn_W2, L0_ffn_b2, L0_ffn_Ws1, L0_ffn_bs1, L0_ffn_Ws2, L0_ffn_bs2)
    return x

_drawn_inputs = setup_inputs


def setup_inputs(seed=0):
    import zlib

    import numpy as np

    out = dict(_drawn_inputs(seed))
    spreads = {'L0_ffn_b1': (0.0, 0.8),
     'L0_ffn_b2': (0.0, 0.516),
     'L0_ffn_bs1': (0.0, 0.312),
     'L0_ffn_bs2': (0.0, 0.1)}
    factors = {'L0_xattn_b': 8.0, 'L0_ffn_W1': 3.363, 'L0_ffn_W2': 3.135}
    for name, (base, spread) in spreads.items():
        noise = np.random.default_rng([zlib.crc32(name.encode()), seed]).standard_normal(out[name].shape)
        drawn = base * np.exp(spread * noise) if base else spread * noise
        out[name] = jnp.asarray(drawn.astype(out[name].dtype))
    for name, factor in factors.items():
        out[name] = (out[name] * factor).astype(out[name].dtype)
    return out
```

```python
from contextlib import ExitStack

import concourse.bass as bass
from concourse import mybir

F32 = mybir.dt.float32
I32 = mybir.dt.int32
U32 = mybir.dt.uint32
ALU = mybir.AluOpType
ACT = mybir.ActivationFunctionType
AX = mybir.AxisListType

P = 128
BANK = 512
EPS = 1e-5
NEG = 1e30
PAD = -3.0e38
CAP_FACTOR = 1.0
MIN_CAP = 8
RSQRT_MAGIC = 1597463007.0
FIRST_BIT = 29


class Signal:

    def __init__(self, sem):
        self.sem, self.value = sem, 0


class Plan:

    def __init__(self):
        self.queues = {name: [] for name in ("tensor", "vector", "scalar", "gpsimd", "sync")}

    def put(self, engine, emit, after=(), signal=None, by=1):
        self.queues[engine].append((emit, list(after), signal.sem if signal else None, by))
        if signal is None:
            return None
        signal.value += by
        return signal, signal.value

    def run(self, engine, eng):
        reached = {}
        for emit, after, sem, by in self.queues[engine]:
            for signal, value in after:
                if reached.get(id(signal), 0) < value:
                    eng.wait_ge(signal.sem, value)
                    reached[id(signal)] = value
            ins = emit(eng)
            if sem is not None:
                ins.then_inc(sem, by)


def xattn_moe_kernel(nc, x, ctx_rows, ctx_mask, Ws, W, w, b, Wcw, bcw, Wcb, bcb,
                     gate, W1, b1, W2, b2, Ws1, bs1, Ws2, bs2, out, xn2_dram):
    B, S, D = x.shape
    T = ctx_rows.shape[1]
    E, _, H = W1.shape
    C = D // P
    M = H // P
    J = S // P
    NT = B * J
    NTOK = B * S
    CAP = max(MIN_CAP, int(CAP_FACTOR * NTOK / E))
    A = CAP // P
    HALVES = S // BANK
    JH = BANK // P
    G = 4
    I = -(-T // G)
    R = G * I
    PAIRS = -(-T // 2)
    BLOCKS = B * PAIRS
    ZB = 3
    XB = 3
    JT = P // E
    NH = NT // JT
    assert D % P == 0 and CAP % P == 0 and HALVES == 2 and I <= 32 and NT % JT == 0 and NH == 2

    plan = Plan()
    put = plan.put

    with ExitStack() as ctx:
        def sb(name, shape, dt=F32):
            return ctx.enter_context(nc.sbuf_tensor(name, shape, dt))

        def signal(name):
            return Signal(ctx.enter_context(nc.semaphore(name)))

        x_ring = sb("x_ring", [P, XB, J, D])
        xn = sb("xn", [P, 2, J, D])
        tr = sb("tr", [P, C, S])
        feat = sb("feat", [P, 2, C, S])
        z = sb("z", [P, ZB, 2 * C * S])
        u = sb("u", [P, M, S])
        w_sb = sb("w_sb", [P, C, D])
        ws_sb = sb("ws_sb", [P, C, D])
        ws1_sb = sb("ws1_sb", [P, C, H])
        ws2_sb = sb("ws2_sb", [P, M, D])
        gate_sb = sb("gate_sb", [P, C, E])
        bs2_rep = sb("bs2_rep", [P, D])
        rho_sb = sb("rho_sb", [P, HALVES, BANK])
        att = sb("att", [P, J, R])
        att_tmp = sb("att_tmp", [P, J, R])
        mask_rep = sb("mask_rep", [P, HALVES, B, R])
        cww_rep = sb("cww_rep", [P, HALVES, B, R])
        cwb_rep = sb("cwb_rep", [P, HALVES, B, R])
        txt_bias = sb("txt_bias", [P, C, B * T])
        window = sb("window", [P, C, 63])
        ident = sb("ident", [P, P])
        ones = sb("ones", [P, P])
        same_expert = sb("same_expert", [P, P])
        earlier_tile = sb("earlier_tile", [P, P])
        expert_of = sb("expert_of", [P, E])
        fold = sb("fold", [P, 32])
        iota_slot = sb("iota_slot", [P, P])
        iota_a = sb("iota_a", [P, A])
        tok_id = sb("tok_id", [P, NT])
        NV = M * E + M + 4 * C
        vec_rows = sb("vec_rows", [NV, P])
        vec = sb("vec", [P, NV])
        bc = sb("bc", [P, 2])
        stats = sb("stats", [P, J, 6])
        mv = sb("mv", [P, J, 2])
        ve = sb("ve", [P, J])
        ry = sb("ry", [P, J])
        ra = sb("ra", [P, J])
        sm = sb("sm", [P, 8, J])
        wb = sb("wb", [P, 2, J])
        lg = sb("lg", [P, J, E])
        probs = sb("probs", [P, NT, E])
        pt = sb("pt", [P, NH * P])
        eq = sb("eq", [P, NH * P])
        gt = sb("gt", [P, NH * P])
        scan = sb("scan", [P, NH * P])
        cur = sb("cur", [P, 4], I32)
        okbit = sb("okbit", [P, 2], I32)
        cnt = sb("cnt", [P, 8])
        off = sb("off", [P, NH])
        slot_i = sb("slot_i", [P, NT * E], I32)
        slot_c = sb("slot_c", [P, NT, E])
        slot_a = sb("slot_a", [P, NT, E])
        pick = sb("pick", [P, 2, NT, 2 * A])
        picked = sb("picked", [P, P])
        idx = sb("idx", [P, 2, A], I32)
        score = sb("score", [P, 2, A])
        y = sb("y", [P, 2, A, D])

        ctx_sb = z[0:T, 2, 0:B * D].rearrange("p (b d) -> p b d", b=B)
        txt_t = z[:, 2, B * D:B * D + C * B * T].rearrange("p (c n) -> p c n", c=C)
        wide = z[:, 2, 2048:2048 + 2 * C * P].rearrange("p (v c m) -> p v c m", v=2, c=C)
        row = z[:, 2, 2560:2560 + 3 * B * R].rearrange("p (v b r) -> p v b r", v=3, b=B)
        mask_i = z[:, 1, 0:B * T].bitcast(I32)
        onehot = feat[:].rearrange("p a c s -> p (a c s)").rearrange("p (t s) -> p t s", t=NT)
        w1_sb = [z[:, n, 0:C * H].rearrange("p (c h) -> p c h", c=C) for n in range(ZB)]
        w2_sb = [z[:, n, C * H:C * H + M * D].rearrange("p (m d) -> p m d", m=M) for n in range(ZB)]
        xg = [xn[:, n, 0:A, :] for n in range(2)]
        xg_t = [xn[:, n, A:2 * A, :].rearrange("p a d -> p (a d)").rearrange("p (c s) -> p c s", c=C)
                for n in range(2)]
        hid = [u[:, n * M // 2:(n + 1) * M // 2, :].rearrange("p m s -> p (m s)")
               .rearrange("p (m s) -> p m s", m=M) for n in range(2)]
        b2_rep = tr[:].rearrange("p c s -> p (c s)").rearrange("p (e d) -> p e d", e=E)

        banks = [ctx.enter_context(nc.psum_tensor(f"bank{i}", [P, BANK], F32)) for i in range(8)]
        rho_ps = banks[0:2]
        up_ps = banks[2:4]
        down_ps = banks[4:6]
        misc_ps = banks[6:8]
        released = {i: [] for i in range(8)}

        loaded = {}

        def load(name, dst, src, after=()):
            s = signal(f"ld_{name}")
            loaded[name] = put("sync", lambda e: e.dma_start(dst, src), after, s, 16)
            return loaded[name]

        pool_const = signal("pool_const")
        pool_add = signal("pool_add")
        v_chain = signal("v_chain")
        v_add = signal("v_add")
        a_tanh = signal("a_tanh")
        a_small = signal("a_small")
        a_gelu = signal("a_gelu")
        t_rho = signal("t_rho")
        t_work = signal("t_work")
        stored = [signal(f"stored{i}") for i in range(B)]
        xn2_stored = [signal(f"xn2_stored{i}") for i in range(B)]
        gathered = [signal(f"gathered{i}") for i in range(2)]
        scattered = signal("scattered")

        def vec_op(emit, *after):
            return put("vector", emit, after, v_chain)

        def pe(emit, *after):
            return put("tensor", emit, after, t_work)

        class Misc:
            turn = 0

        def misc_bank():
            n = 6 + Misc.turn % 2
            Misc.turn += 1
            return n

        def load_x(batch, after=()):
            xr = x[batch].rearrange("(j p) d -> p j d", p=P)
            return load(f"x{batch}", x_ring[:, batch % XB], xr, after)

        load_x(0)
        load("w", w_sb[:], W.rearrange("(c p) d -> p c d", p=P))
        load("ctx", ctx_sb, ctx_rows.rearrange("b t d -> t b d"))
        load("ws", ws_sb[:], Ws.rearrange("(c p) d -> p c d", p=P))
        vec_sources = [("b1", b1.rearrange("e (m p) -> (e m) p", p=P)),
                       ("bs1", bs1.rearrange("(m p) -> m p", p=P)),
                       ("b", b.rearrange("a (c p) -> (a c) p", p=P)),
                       ("Wcw", Wcw.rearrange("a (c p) -> (a c) p", p=P)),
                       ("Wcb", Wcb.rearrange("a (c p) -> (a c) p", p=P)),
                       ("w_col", w.rearrange("(c p) a -> (c a) p", p=P))]
        at, col = 0, {}
        for name, src in vec_sources:
            n = src.shape[0]
            load("v_" + name, vec_rows[at:at + n, :], src)
            col[name] = at
            at += n
        assert at == NV
        load("mask", mask_i, ctx_mask.rearrange("b t -> (b t)").partition_broadcast(P))
        load("bcw", bc[:, 0:1], bcw.partition_broadcast(P))
        load("bcb", bc[:, 1:2], bcb.partition_broadcast(P))
        load("gate", gate_sb[:], gate.rearrange("(c p) e -> p c e", p=P))
        load("bs2", bs2_rep[:], bs2.partition_broadcast(P))
        load_x(1)
        load("ws1", ws1_sb[:], Ws1.rearrange("(c p) h -> p c h", p=P))
        load("ws2", ws2_sb[:], Ws2.rearrange("(m p) d -> p m d", p=P))
        load_x(2)

        def const(emit, *after):
            return put("gpsimd", emit, after, pool_const)

        c0 = const(lambda e: e.memset(ident[:], 0.0))
        ident_ok = const(lambda e: e.affine_select(out=ident[:], in_=ident[:], compare_op=ALU.not_equal, fill=1.0,
                                                   base=0, pattern=[[-1, P]], channel_multiplier=1), c0)
        ones_ok = const(lambda e: e.memset(ones[:], 1.0))
        const(lambda e: e.iota(iota_slot[:], [[1, P]], base=0, channel_multiplier=0,
                               allow_small_or_imprecise_dtypes=True))
        const(lambda e: e.iota(iota_a[:], [[1, A]], base=0, channel_multiplier=0,
                               allow_small_or_imprecise_dtypes=True))
        iota_ok = const(lambda e: e.iota(tok_id[:], [[P, NT]], base=0, channel_multiplier=1,
                                         allow_small_or_imprecise_dtypes=True))
        row_ok = const(lambda e: e.memset(row, 0.0))
        win0 = const(lambda e: e.memset(window[:], 0.0))

        def layer_norm(src, dst, *after):
            for j in range(J):
                t = vec_op(lambda e, j=j: e.bn_stats(stats[:, j, :], src[:, j, :]), *after)
            for j in range(J):
                t2 = vec_op(lambda e, j=j: e.bn_aggr(mv[:, j, :], stats[:, j, :]), t)
            t = vec_op(lambda e: e.tensor_scalar(ve[:], mv[:, :, 1], EPS, None, ALU.add), t2)
            t = vec_op(lambda e: e.tensor_scalar(ry[:].bitcast(I32), ve[:].bitcast(I32), 1, None,
                                                 ALU.logical_shift_right), t)
            t = vec_op(lambda e: e.tensor_scalar(ry[:].bitcast(I32), ry[:].bitcast(I32), -1.0, RSQRT_MAGIC,
                                                 ALU.mult, ALU.add), t)
            for _ in range(4):
                t = vec_op(lambda e: e.scalar_tensor_tensor(out=ra[:], in0=ry[:], scalar=-0.5, in1=ry[:],
                                                            op0=ALU.mult, op1=ALU.mult), t)
                t = vec_op(lambda e: e.tensor_tensor(ra[:], ra[:], ve[:], ALU.mult), t)
                t = vec_op(lambda e: e.scalar_tensor_tensor(out=ry[:], in0=ra[:], scalar=1.5, in1=ry[:],
                                                            op0=ALU.add, op1=ALU.mult), t)
            return t

        def normalise(src, dst, t, *after):
            for j in range(J):
                t2 = vec_op(lambda e, j=j: e.tensor_scalar(dst[:, j, :], src[:, j, :], mv[:, j, 0:1], ry[:, j:j + 1],
                                                           ALU.subtract, ALU.mult), t, *after)
            return t2

        xn_ready, xn2_ready, feat_ready, tr_ready = {}, {}, {}, {}
        tr_free = []
        xn_free = {0: [], 1: []}
        last_tanh, rho_done, x2_ready = {}, {}, {}

        def transpose_tiles(src, ready, quarter):
            c, h = quarter // HALVES, quarter % HALVES
            n = misc_bank()
            bank = banks[n]

            def four(e):
                for j in range(JH):
                    ins = e.transpose(bank[:, j * P:(j + 1) * P], src[:, h * JH + j, c * P:(c + 1) * P], ident[:])
                return ins

            t = pe(four, ready, ident_ok, *released[n])
            done = vec_op(lambda e: e.tensor_copy(tr[:, c, h * BANK:(h + 1) * BANK], bank[:]), t, *tr_free)
            released[n] = [done]
            return done

        SLOT = "next slot"

        def pre_steps(batch):
            src, dst = x_ring[:, batch % XB], xn[:, batch % 2]
            hold = {}

            def norm():
                hold["rstd"] = layer_norm(src, dst, loaded[f"x{batch}"])

            def apply():
                xn_ready[batch] = normalise(src, dst, hold["rstd"], *xn_free[batch % 2])

            yield norm
            yield SLOT
            yield apply
            yield SLOT
            copies = []
            for q in range(C * HALVES):
                yield lambda q=q: copies.append(transpose_tiles(dst, xn_ready[batch], q))
                yield SLOT
            for co in range(C):
                for h in range(HALVES):
                    def project(co=co, h=h):
                        n = misc_bank()
                        bank = banks[n]

                        def mm(e):
                            for c in range(C):
                                ins = e.matmul(bank[:], w_sb[:, c, co * P:(co + 1) * P],
                                               tr[:, c, h * BANK:(h + 1) * BANK], start=c == 0, stop=c == C - 1)
                            return ins

                        t = pe(mm, copies[-1], loaded["w"], *released[n])
                        done = vec_op(lambda e: e.tensor_copy(feat[:, batch % 2, co, h * BANK:(h + 1) * BANK],
                                                              bank[:]), t, *feat_free[batch % 2])
                        released[n] = [done]
                        feat_ready[batch] = done
                        tr_free[:] = [t]
                    yield project
                    yield SLOT

        feat_free = {0: [], 1: []}
        z_free = {n: [] for n in range(ZB)}
        added, tanhed = {}, {}

        def block_of(n):
            batch, k = n // PAIRS, n % PAIRS
            return batch, k, [t for t in (2 * k, 2 * k + 1) if t < T]

        def add_block(n):
            batch, k, rows = block_of(n)
            zb = z[:, n % ZB, :].rearrange("p (e c s) -> p e c s", e=2, c=C)
            done = []
            for r, t in enumerate(rows):
                for c in range(C):
                    emit = lambda e, r=r, t=t, c=c: e.tensor_scalar(
                        zb[:, r, c, :], feat[:, batch % 2, c, :], txt_bias[:, c, batch * T + t:batch * T + t + 1],
                        None, ALU.add)
                    after = [feat_ready[batch], txt_ready[0], *z_free[n % ZB]]
                    if r == 1 and c == C - 1:
                        done.append(put("gpsimd", emit, after, pool_add))
                    else:
                        tok = put("vector", emit, after, v_add)
                        done = [d for d in done if d[0] is not v_add] + [tok]
            added[n] = done
            if k == PAIRS - 1:
                feat_free[batch % 2] = done

        def tanh_block(n):
            _, _, rows = block_of(n)
            part = z[:, n % ZB, 0:len(rows) * C * S]
            tanhed[n] = put("scalar", lambda e: e.activation(part, part, ACT.Tanh), added[n], a_tanh)

        def rho_block(n):
            batch, k, rows = block_of(n)
            zb = z[:, n % ZB, :].rearrange("p (e c s) -> p e c s", e=2, c=C)

            def mm(e):
                for c in range(C):
                    for h in range(HALVES):
                        for r, t in enumerate(rows):
                            g = (t + 2 * h) % G
                            i = t // G
                            ins = e.matmul(rho_ps[h][32 * g:32 * g + 32, :], window[:, c, 31 - i:63 - i],
                                           zb[:, r, c, h * BANK:(h + 1) * BANK],
                                           start=(c == 0 and i == 0), stop=(c == C - 1 and t + G >= T))
                return ins

            tok = put("tensor", mm, [tanhed[n], window_ready[0], *released[0], *released[1]], t_rho)
            z_free[n % ZB] = [tok]
            rho_done[n] = tok

        def tail_steps(batch):
            last = rho_done[batch * PAIRS + PAIRS - 1]
            xs, ns = x_ring[:, batch % XB], xn[:, batch % 2]
            hold = {}

            def evacuate():
                for h in range(HALVES):
                    t = vec_op(lambda e, h=h: e.tensor_copy(rho_sb[:, h, :], rho_ps[h][:]), last, *hold.get("rho_sb", []))
                    released[h] = [t]
                hold["rho"] = t
            yield evacuate

            def to_tokens():
                hold["rt"] = []
                for h in range(HALVES):
                    n = misc_bank()

                    def four(e, h=h, n=n):
                        for j in range(JH):
                            ins = e.transpose(banks[n][:, j * P:(j + 1) * P], rho_sb[:, h, j * P:(j + 1) * P], ident[:])
                        return ins
                    hold["rt"].append((n, pe(four, hold["rho"], *released[n])))
            yield to_tokens
            yield SLOT

            def shift():
                for h, (n, t) in enumerate(hold["rt"]):
                    rt = banks[n][:].rearrange("p (j g i) -> p j g i", j=JH, g=G)
                    for j in range(JH):
                        dst = att[:, h * JH + j, :].rearrange("p (g i) -> p g i", g=G)
                        m = mask_rep[:, h, batch, :].rearrange("p (g i) -> p g i", g=G)
                        t2 = vec_op(lambda e, dst=dst, j=j, rt=rt, m=m: e.tensor_tensor(
                            dst, rt[:, j, :, 0:I], m, ALU.add), t)
                    released[n] = [t2]
                t = vec_op(lambda e: e.tensor_reduce(sm[:, 0, :], att[:], AX.X, ALU.max), t2)
                hold["e"] = vec_op(lambda e: e.tensor_tensor(
                    att[:], att[:], sm[:, 0, :].unsqueeze(2).broadcast_to([P, J, R]), ALU.subtract), t)
            yield shift
            yield SLOT

            def exp():
                hold["e"] = put("scalar", lambda e: e.activation(att[:], att[:], ACT.Exp), [hold["e"]], a_small)
            yield exp
            yield SLOT

            def weigh():
                t = hold["e"]
                vec_op(lambda e: e.tensor_reduce(sm[:, 1, :], att[:], AX.X, ALU.add), t)
                for v, rep in enumerate((cww_rep, cwb_rep)):
                    for h in range(HALVES):
                        t = vec_op(lambda e, rep=rep, h=h: e.tensor_tensor(
                            att_tmp[:, h * JH:(h + 1) * JH, :], att[:, h * JH:(h + 1) * JH, :],
                            rep[:, h, batch, :].unsqueeze(1).broadcast_to([P, JH, R]), ALU.mult), t)
                    t = vec_op(lambda e, v=v: e.tensor_reduce(wb[:, v, :], att_tmp[:], AX.X, ALU.add), t)
                t = vec_op(lambda e: e.reciprocal(sm[:, 2, :], sm[:, 1, :]), t)
                for v in range(2):
                    t2 = vec_op(lambda e, v=v: e.tensor_tensor(wb[:, v, :], wb[:, v, :], sm[:, 2, :], ALU.mult), t)
                for v in range(2):
                    t = vec_op(lambda e, v=v: e.tensor_scalar(wb[:, v, :], wb[:, v, :], bc[:, v:v + 1], None, ALU.add),
                               t2, loaded["bcw"], loaded["bcb"])
                hold["wb"] = t
            yield weigh
            yield SLOT

            def gates():
                hold["wb"] = put("scalar", lambda e: e.activation(wb[:], wb[:], ACT.Tanh), [hold["wb"]], a_small)
            yield gates
            yield SLOT

            def residual():
                for j in range(J):
                    t = vec_op(lambda e, j=j: e.tensor_scalar(ns[:, j, :], ns[:, j, :], wb[:, 0, j:j + 1],
                                                              wb[:, 1, j:j + 1], ALU.mult, ALU.add), hold["wb"])
                hold["x2"] = vec_op(lambda e: e.tensor_tensor(xs, xs, ns, ALU.add), t)
            yield residual
            yield SLOT

            def norm():
                hold["rstd"] = layer_norm(xs, ns, hold["x2"])
            yield norm
            yield SLOT

            def apply():
                t = normalise(xs, ns, hold["rstd"])
                xn2_ready[batch] = t
                x2_ready[batch] = vec_op(lambda e: e.tensor_tensor(
                    xs, xs, bs2_rep[:].unsqueeze(1).broadcast_to([P, J, D]), ALU.add), t, loaded["bs2"])
                hold["store"] = put("sync", lambda e: e.dma_start(
                    xn2_dram[batch * S:(batch + 1) * S, :].rearrange("(j p) d -> p j d", p=P), ns),
                    [t], xn2_stored[batch], 16)
            yield apply
            yield SLOT
            hold["copies"] = []
            for q in range(C * HALVES):
                def tq(q=q):
                    hold["copies"].append(transpose_tiles(ns, xn2_ready[batch], q))
                    tr_ready[batch] = hold["copies"][-1]
                    xn_free[batch % 2] = [hold["copies"][-1], hold["store"]]
                yield tq
                yield SLOT

            def logits():
                n = misc_bank()

                def mm(e):
                    for j in range(J):
                        for c in range(C):
                            ins = e.matmul(banks[n][:, j * E:(j + 1) * E], tr[:, c, j * P:(j + 1) * P],
                                           gate_sb[:, c, :], start=c == 0, stop=c == C - 1)
                    return ins
                hold["lg"] = (n, pe(mm, tr_ready[batch], loaded["gate"], *released[n]))
            yield logits
            yield SLOT

            def shift_logits():
                n, t = hold["lg"]
                lp = banks[n][:, 0:J * E].rearrange("p (j e) -> p j e", j=J)
                t = vec_op(lambda e: e.tensor_reduce(sm[:, 3, :], lp, AX.X, ALU.max), t)
                t = vec_op(lambda e: e.tensor_tensor(lg[:], lp, sm[:, 3, :].unsqueeze(2).broadcast_to([P, J, E]),
                                                     ALU.subtract), t)
                released[n] = [t]
                hold["lg"] = t
            yield shift_logits
            yield SLOT

            def exp_logits():
                hold["lg"] = put("scalar", lambda e: e.activation(lg[:], lg[:], ACT.Exp), [hold["lg"]], a_small)
            yield exp_logits
            yield SLOT

            def router():
                t = vec_op(lambda e: e.tensor_reduce(sm[:, 4, :], lg[:], AX.X, ALU.add), hold["lg"])
                t = vec_op(lambda e: e.reciprocal(sm[:, 5, :], sm[:, 4, :]), t)
                probs_ready[batch] = vec_op(lambda e: e.tensor_tensor(
                    probs[:, batch * J:(batch + 1) * J, :], lg[:], sm[:, 5, :].unsqueeze(2).broadcast_to([P, J, E]),
                    ALU.mult), t)
            yield router

        probs_ready = {}
        up_turn, down_turn = [0], [0]
        u_free = []

        def shared_up(batch, h, m, direct):
            n = 2 + up_turn[0] % 2
            up_turn[0] += 1

            def mm(e):
                for c in range(C):
                    ins = e.matmul(banks[n][:], ws1_sb[:, c, m * P:(m + 1) * P], tr[:, c, h * BANK:(h + 1) * BANK],
                                   start=c == 0, stop=c == C - 1)
                return ins
            t = pe(mm, tr_ready[batch], loaded["ws1"], *released[n])
            tr_free[:] = [t]
            dst, bias = u[:, m, h * BANK:(h + 1) * BANK], vec[:, col["bs1"] + m:col["bs1"] + m + 1]
            if direct:
                done = put("scalar", lambda e: e.activation(dst, banks[n][:], ACT.Gelu_apprx_tanh, bias=bias),
                           [t, vec_ready[0], *u_free], a_gelu)
            else:
                done = vec_op(lambda e: e.tensor_scalar(dst, banks[n][:], bias, None, ALU.add),
                              t, vec_ready[0], *u_free)
            released[n] = [done]
            return done

        def shared_down(batch, j, ready):
            n = 4 + down_turn[0] % 2
            down_turn[0] += 1
            xs = x_ring[:, batch % XB, j, :]

            def mm(e):
                for m in range(M):
                    ins = e.matmul(banks[n][:, 0:D], u[:, m, j * P:(j + 1) * P], ws2_sb[:, m, :],
                                   start=m == 0, stop=m == M - 1)
                return ins
            t = pe(mm, ready, loaded["ws2"], *released[n])
            done = vec_op(lambda e: e.tensor_tensor(xs, banks[n][:, 0:D], xs, ALU.add), t, x2_ready[batch])
            released[n] = [done]
            return t, done

        def store_batch(batch, ready):
            xs = x_ring[:, batch % XB]
            t = put("sync", lambda e: e.dma_start(out[batch].rearrange("(j p) d -> p j d", p=P), xs),
                    [ready], stored[batch], 16)
            if batch + XB < B:
                load_x(batch + XB, [t])

        def shared_steps(batch):
            hold = {}
            for h in range(HALVES):
                for m in range(M):
                    def up(h=h, m=m):
                        hold[h] = shared_up(batch, h, m, False)
                    yield up
                    yield SLOT
                def gelu(h=h):
                    part = u[:, :, h * BANK:(h + 1) * BANK]
                    hold["g", h] = put("scalar", lambda e: e.activation(part, part, ACT.Gelu_apprx_tanh),
                                       [hold[h]], a_gelu)
                if h == HALVES - 1:
                    yield SLOT
                    for hh in range(HALVES):
                        yield lambda hh=hh: gelu(hh)
                    yield SLOT
            for j in range(J):
                def down(j=j):
                    t, done = shared_down(batch, j, hold["g", j // JH])
                    u_free[:] = [t]
                    if j == J - 1:
                        store_batch(batch, done)
                yield down
                yield SLOT

        def transposed(n, dst, src, rows, cols, at, *after):
            return pe(lambda e: e.transpose(banks[n][0:cols, at:at + rows], src, ident[0:rows, 0:rows]),
                      ident_ok, *after, *released[n])

        for step in pre_steps(0):
            if step is not SLOT:
                step()

        t = pe(lambda e: e.transpose(up_ps[0][:, 0:NV], vec_rows[:], ident[0:NV, 0:NV]), ident_ok,
               *[loaded["v_" + name] for name, _ in vec_sources])
        vec_ready = [vec_op(lambda e: e.tensor_copy(vec[:], up_ps[0][:, 0:NV]), t)]
        released[2] = vec_ready[:]
        t = vec_op(lambda e: e.tensor_copy(window[:, :, 31], vec[:, col["w_col"]:col["w_col"] + C]),
                   vec_ready[0], win0)
        window_ready = [t]

        def ctx_transposes(e, c):
            for bb in range(B):
                ins = e.transpose(down_ps[c][:, bb * T:(bb + 1) * T], ctx_sb[:, bb, c * P:(c + 1) * P],
                                  ident[0:T, 0:T])
            return ins
        for c in range(C):
            t = pe(lambda e, c=c: ctx_transposes(e, c), loaded["ctx"], ident_ok)
            t = vec_op(lambda e, c=c: e.tensor_copy(txt_t[:, c, :], down_ps[c][:, 0:B * T]), t)
            released[4 + c] = [t]
        txt_t_ready = t
        for co in range(C):
            def mm(e, co=co):
                for c in range(C):
                    ins = e.matmul(up_ps[co][:, 0:B * T], ws_sb[:, c, co * P:(co + 1) * P], txt_t[:, c, :],
                                   start=c == 0, stop=c == C - 1)
                return ins
            t = pe(mm, txt_t_ready, loaded["ws"], *released[2 + co])
            t = vec_op(lambda e, co=co: e.tensor_scalar(txt_bias[:, co, :], up_ps[co][:, 0:B * T],
                                                        vec[:, col["b"] + co:col["b"] + co + 1], None, ALU.add), t,
                       vec_ready[0])
            released[2 + co] = [t]
        txt_ready = [t]

        for v, name in enumerate(("Wcw", "Wcb")):
            for c in range(C):
                t = vec_op(lambda e, v=v, c=c, name=name: e.tensor_scalar(
                    wide[:, v, c, :], ones[:], vec[:, col[name] + c:col[name] + c + 1], None, ALU.mult),
                    vec_ready[0], ones_ok)
        wide_ready = t
        t = vec_op(lambda e: e.tensor_scalar(row[:, 0, :, 0:T], mask_i.rearrange("p (b t) -> p b t", b=B), 1.0, NEG,
                                             ALU.subtract, ALU.mult), loaded["mask"], row_ok)
        if R > T:
            t = vec_op(lambda e: e.memset(row[:, 0, :, T:R], PAD), row_ok)
        for v in range(2):
            def mm(e, v=v):
                for c in range(C):
                    ins = e.matmul(down_ps[v][:, 0:B * T], wide[:, v, c, :], txt_t[:, c, :],
                                   start=c == 0, stop=c == C - 1)
                return ins
            t = pe(mm, wide_ready, txt_t_ready, *released[4 + v])
            t = vec_op(lambda e, v=v: e.tensor_copy(row[:, 1 + v, :, 0:T],
                                                    down_ps[v][:, 0:B * T].rearrange("p (b t) -> p b t", b=B)),
                       t, row_ok)
            released[4 + v] = [t]
        for v, rep in enumerate((mask_rep, cww_rep, cwb_rep)):
            for h in range(HALVES):
                for g in range(G):
                    src = row[:, v, :, :].rearrange("p b (i g) -> p b g i", g=G)[:, :, g, :]
                    dst = rep[:, h, :, :].rearrange("p b (g i) -> p b g i", g=G)[:, :, (g + 2 * h) % G, :]
                    t2 = vec_op(lambda e, dst=dst, src=src: e.tensor_copy(dst, src), t)
        setup_done = t2
        z_free[1] = [setup_done]
        z_free[2] = [setup_done]

        t = vec_op(lambda e: e.tensor_reduce(expert_of[:], ident[:].rearrange("p (t e) -> p e t", e=E), AX.X, ALU.add),
                   ident_ok)
        vec_op(lambda e: e.tensor_reduce(fold[:], ident[:].rearrange("p (g r) -> p r g", r=32), AX.X, ALU.add),
               ident_ok)
        t = vec_op(lambda e: e.tensor_copy(same_expert[:].rearrange("p (t e) -> p t e", e=E),
                                           expert_of[:].unsqueeze(1).broadcast_to([P, JT, E])), t)
        router_consts = t
        earlier_ok = const(lambda e: e.affine_select(out=earlier_tile[:], in_=same_expert[:], compare_op=ALU.is_gt,
                                                     fill=0.0, base=0, pattern=[[1, P]], channel_multiplier=-1), t)

        add_block(0)
        tanh_block(0)
        add_block(1)
        background = []
        for n in range(BLOCKS):
            batch, k, _ = block_of(n)
            if k == 0:
                background = []
                if batch > 0:
                    background += list(tail_steps(batch - 1)) + [SLOT] + list(shared_steps(batch - 1))
                if batch + 1 < B:
                    background += list(pre_steps(batch + 1))
                slots = background.count(SLOT) + 1
                per_slot = -(-slots // (PAIRS - 3))
            if n + 2 < BLOCKS:
                if (n + 2) % PAIRS == 0:
                    while background:
                        step = background.pop(0)
                        if step is not SLOT:
                            step()
                add_block(n + 2)
            if n + 1 < BLOCKS:
                tanh_block(n + 1)
            if k == 0 and batch > 0:
                background.pop(0)()
            rho_block(n)
            for _ in range(per_slot):
                while background:
                    step = background.pop(0)
                    if step is SLOT:
                        break
                    step()

        last = B - 1
        for step in tail_steps(last):
            if step is not SLOT:
                step()
        all_tanh = tanhed[BLOCKS - 1]
        all_rho = rho_done[BLOCKS - 1]

        def load_expert(ex, *after):
            n = ex % ZB
            load(f"w1_{ex}", w1_sb[n], W1[ex].rearrange("(c p) h -> p c h", p=P), after)
            load(f"w2_{ex}", w2_sb[n], W2[ex].rearrange("(m p) d -> p m d", p=P), after)

        for ex in range(ZB):
            load_expert(ex, all_rho)

        filler = []
        ups = {}
        for h in range(HALVES):
            for m in range(M):
                def up(h=h, m=m):
                    ups[h] = shared_up(last, h, m, True)
                filler.append(up)
        for j in range(J):
            def down(j=j):
                t, done = shared_down(last, j, ups[j // JH])
                u_free[:] = [t]
                if j == J - 1:
                    store_batch(last, done)
            filler.append(down)

        def fill():
            if filler:
                filler.pop(0)()

        for hf in range(NH):
            n = 6 + hf
            t = pe(lambda e, hf=hf, n=n: e.transpose(
                banks[n][:, 0:P], probs[:, hf * JT:(hf + 1) * JT, :].rearrange("p t e -> p (t e)"), ident[:]),
                probs_ready[last], *released[n])
            t = vec_op(lambda e, hf=hf, n=n: e.tensor_copy(pt[:, hf * P:(hf + 1) * P], banks[n][:, 0:P]), t)
            released[n] = [t]
        pt_ready = t
        cur_i, cand_i = cur[:, 0:1], cur[:, 1:2]
        vec_op(lambda e: e.memset(cur_i, 0))
        t = vec_op(lambda e: e.memset(cand_i, 1 << FIRST_BIT))
        cand_ready = t
        tot_ps = rho_ps[0]
        for bit in range(FIRST_BIT, -1, -1):
            t = vec_op(lambda e: e.tensor_scalar(gt[:], pt[:], cand_i.bitcast(F32), None, ALU.is_ge, ALU.add,
                                                 accum_out=cnt[:, 0:1]), cand_ready, pt_ready)
            t = pe(lambda e: e.matmul(tot_ps[:, 0:1], same_expert[:], cnt[:, 0:1], start=True, stop=True),
                   t, router_consts, *released[0])
            if bit % 2:
                fill()
            t = vec_op(lambda e, bit=bit: e.tensor_scalar(okbit[:, 0:1], tot_ps[:, 0:1], float(CAP), float(1 << bit),
                                                          ALU.is_ge, ALU.mult), t)
            released[0] = [t]
            if bit:
                t2 = vec_op(lambda e, bit=bit: e.scalar_tensor_tensor(
                    out=cand_i, in0=okbit[:, 0:1], scalar=1 << (bit - 1), in1=cur_i, op0=ALU.bitwise_or,
                    op1=ALU.bitwise_or), t)
                cand_ready = t2
            cur_ready = vec_op(lambda e: e.tensor_tensor(cur_i, okbit[:, 0:1], cur_i, ALU.bitwise_or), t, *([t2] if bit else []))

        thr = cur_i.bitcast(F32)
        t = vec_op(lambda e: e.tensor_scalar(gt[:], pt[:], thr, None, ALU.is_gt, ALU.add, accum_out=cnt[:, 0:1]),
                   cur_ready)
        t_above = t
        t = pe(lambda e: e.matmul(tot_ps[:, 0:1], same_expert[:], cnt[:, 0:1], start=True, stop=True), t,
               *released[0])
        fill()
        t_eq = vec_op(lambda e: e.tensor_scalar(eq[:], pt[:], thr, None, ALU.is_equal), t_above)
        left = vec_op(lambda e: e.tensor_scalar(cnt[:, 1:2], tot_ps[:, 0:1], -1.0, float(CAP), ALU.mult, ALU.add), t)
        released[0] = [left]

        def ranks(src, ready):
            for hf in range(NH):
                part = slice(hf * P, (hf + 1) * P)
                t = vec_op(lambda e, part=part: e.tensor_tensor_scan(scan[:, part], src[:, part], src[:, part], 0.0,
                                                                     ALU.add, ALU.bypass), ready)
            for hf in range(NH):
                t2 = vec_op(lambda e, hf=hf: e.tensor_copy(cnt[:, 2 + hf:3 + hf], scan[:, hf * P + P - 1:hf * P + P]), t)

            def mm(e):
                e.matmul(tot_ps[:, 0:1], earlier_tile[:], cnt[:, 2:3], start=True, stop=True)
                e.matmul(tot_ps[:, 1:2], same_expert[:], cnt[:, 2:3], start=True, stop=False)
                return e.matmul(tot_ps[:, 1:2], earlier_tile[:], cnt[:, 3:4], start=False, stop=True)
            t = pe(mm, t2, earlier_ok, *released[0])
            fill()
            t = vec_op(lambda e: e.tensor_copy(off[:], tot_ps[:, 0:NH]), t)
            released[0] = [t]
            return t

        t = ranks(eq, t_eq)
        for hf in range(NH):
            part = slice(hf * P, (hf + 1) * P)
            t2 = vec_op(lambda e, part=part, hf=hf: e.tensor_scalar(scan[:, part], scan[:, part], off[:, hf:hf + 1],
                                                                    cnt[:, 1:2], ALU.add, ALU.is_le), t, left)
        t = vec_op(lambda e: e.tensor_tensor(eq[:], eq[:], scan[:], ALU.mult), t2)
        chosen = vec_op(lambda e: e.tensor_tensor(gt[:], gt[:], eq[:], ALU.add), t)
        t = ranks(gt, chosen)
        for hf in range(NH):
            part = slice(hf * P, (hf + 1) * P)
            t2 = vec_op(lambda e, part=part, hf=hf: e.scalar_tensor_tensor(
                out=scan[:, part], in0=scan[:, part], scalar=off[:, hf:hf + 1], in1=gt[:, part], op0=ALU.add,
                op1=ALU.mult), t)
        n = 6
        t = pe(lambda e: [e.transpose(banks[n][:, hf * P:(hf + 1) * P], scan[:, hf * P:(hf + 1) * P], ident[:])
                          for hf in range(NH)][-1], t2, *released[n])
        fill()
        t = vec_op(lambda e: e.tensor_scalar(slot_i[:], banks[n][:, 0:NT * E], -1.0, None, ALU.add), t)
        released[n] = [t]
        sc_v = slot_c[:].rearrange("p t e -> p (t e)")
        sa_v = slot_a[:].rearrange("p t e -> p (t e)")
        t3 = vec_op(lambda e: e.tensor_scalar(eq[:].bitcast(I32), slot_i[:], P - 1, None, ALU.bitwise_and), t)
        t4 = vec_op(lambda e: e.tensor_scalar(gt[:].bitcast(I32), slot_i[:], 7, None, ALU.arith_shift_right), t)
        t5 = vec_op(lambda e: e.tensor_copy(sc_v, eq[:].bitcast(I32)), t3)
        slots_ready = vec_op(lambda e: e.tensor_copy(sa_v, gt[:].bitcast(I32)), t4, t5)

        list_ps, slot_ps = banks[1], banks[0]
        released[1] = [vec_op(lambda e: e.memset(list_ps[:], 0.0), *released[1])]
        b2_loaded = None
        pick_free, onehot_free, picked_free = {0: [], 1: []}, [all_tanh], []
        idx_free, score_free = {0: [], 1: []}, {0: [], 1: []}
        xg_free = {0: [probs_ready[last]], 1: [probs_ready[last]]}
        xgt_free, hid_free, y_free = {0: [], 1: []}, {0: [], 1: []}, {0: [], 1: []}
        listed, gathers, scatters = {}, {}, {}

        def make_list(ex):
            k = ex % 2
            sa = slot_a[:, :, ex:ex + 1].broadcast_to([P, NT, A])
            t = vec_op(lambda e: e.tensor_tensor(pick[:, k, :, A:2 * A], sa,
                                                 iota_a[:].unsqueeze(1).broadcast_to([P, NT, A]), ALU.is_equal),
                       slots_ready, iota_ok, *pick_free[k])
            t2 = vec_op(lambda e: e.tensor_tensor(pick[:, k, :, 0:A], pick[:, k, :, A:2 * A],
                                                  tok_id[:].unsqueeze(2).broadcast_to([P, NT, A]), ALU.mult), t)
            t3 = vec_op(lambda e: e.tensor_tensor(pick[:, k, :, A:2 * A], pick[:, k, :, A:2 * A],
                                                  probs[:, :, ex:ex + 1].broadcast_to([P, NT, A]), ALU.mult), t2)
            t4 = vec_op(lambda e: e.tensor_tensor(onehot, slot_c[:, :, ex:ex + 1].broadcast_to([P, NT, P]),
                                                  iota_slot[:].unsqueeze(1).broadcast_to([P, NT, P]), ALU.is_equal),
                        *onehot_free)

            def mm(e):
                for tile in range(NT):
                    g = tile % G
                    ins = e.matmul(list_ps[32 * g:32 * g + 2 * A, 0:P], pick[:, k, tile, :], onehot[:, tile, :],
                                   start=tile < G, stop=tile >= NT - G, skip_group_check=True)
                return ins
            t = pe(mm, t3, t4, *released[1])
            pick_free[k], onehot_free[:] = [t], [t]
            t = vec_op(lambda e: e.tensor_copy(picked[:], list_ps[:, 0:P]), t, *picked_free)
            released[1] = [t]
            t = pe(lambda e: e.matmul(slot_ps[:, 0:2 * A], picked[:], fold[:, 0:2 * A], start=True, stop=True), t,
                   *released[0])
            picked_free[:] = [t]
            vec_op(lambda e: e.tensor_copy(idx[:, k, :], slot_ps[:, 0:A]), t, *idx_free[k])
            t = vec_op(lambda e: e.tensor_copy(score[:, k, :], slot_ps[:, A:2 * A]), t, *score_free[k])
            released[0] = [t]
            listed[ex] = t

        def gather(ex):
            k = ex % 2
            for a in range(A):
                off_ap = bass.IndirectOffsetOnAxis(idx[:, k, a:a + 1].bitcast(U32), 0)
                t = put("gpsimd", lambda e, a=a, off_ap=off_ap: e.indirect_dma_start(
                    xg[k][:, a, :], None, xn2_dram[:, :], off_ap),
                    [listed[ex], *xg_free[k], *[(s, 16) for s in xn2_stored]], gathered[k], 16)
            gathers[ex] = t

        def turn_gathered(ex):
            k = ex % 2
            for c in range(C):
                n = misc_bank()

                def four(e, c=c, n=n):
                    for a in range(A):
                        ins = e.transpose(banks[n][:, a * P:(a + 1) * P], xg[k][:, a, c * P:(c + 1) * P], ident[:])
                    return ins
                t = pe(four, gathers[ex], *released[n])
                t2 = vec_op(lambda e, c=c, n=n: e.tensor_copy(xg_t[k][:, c, :], banks[n][:]), t, *xgt_free[k])
                released[n] = [t2]
            xg_free[k] = [t]
            return t2

        hid_ready = {}

        def expert_up(ex, ready):
            k = ex % 2
            wk = ex % ZB
            for m in range(M):
                n = 2 + up_turn[0] % 2
                up_turn[0] += 1

                def mm(e, m=m, n=n):
                    for c in range(C):
                        ins = e.matmul(banks[n][:], w1_sb[wk][:, c, m * P:(m + 1) * P], xg_t[k][:, c, :],
                                       start=c == 0, stop=c == C - 1)
                    return ins
                t = pe(mm, ready, loaded[f"w1_{ex}"], *released[n])
                cb = col["b1"] + ex * M + m
                t2 = put("scalar", lambda e, m=m, n=n, cb=cb: e.activation(hid[k][:, m, :], banks[n][:],
                                                                         ACT.Gelu_apprx_tanh, bias=vec[:, cb:cb + 1]),
                         [t, *hid_free[k]], a_gelu)
                released[n] = [t2]
                hid_ready[ex, m] = t2
            xgt_free[k] = [t]

        def expert_down(ex):
            k = ex % 2
            wk = ex % ZB
            rows = []
            for a in range(A):
                n = 4 + down_turn[0] % 2
                down_turn[0] += 1
                for m in range(M):
                    t = pe(lambda e, a=a, m=m, n=n: e.matmul(banks[n][:, 0:D], hid[k][:, m, a * P:(a + 1) * P],
                                                             w2_sb[wk][:, m, :], start=m == 0, stop=m == M - 1),
                           hid_ready[ex, m], loaded[f"w2_{ex}"], *released[n])
                t = vec_op(lambda e, a=a, n=n: e.tensor_tensor(y[:, k, a, :], banks[n][:, 0:D], b2_rep[:, ex, :],
                                                               ALU.add), t, b2_loaded, *y_free[k])
                released[n] = [t]
                rows.append(vec_op(lambda e, a=a: e.tensor_scalar(y[:, k, a, :], y[:, k, a, :], score[:, k, a:a + 1],
                                                                  None, ALU.mult), t))
            hid_free[k] = [(t_work, t_work.value)]
            score_free[k] = [rows[-1]]
            before = [scatters[ex - 1]] if ex else [(s, 16) for s in stored]
            for a in range(A):
                off_ap = bass.IndirectOffsetOnAxis(idx[:, k, a:a + 1].bitcast(U32), 0)
                t = put("gpsimd", lambda e, a=a, off_ap=off_ap: e.indirect_dma_start(
                    out_rows, off_ap, y[:, k, a, :], None, compute_op=ALU.add), [rows[a], *before], scattered, 16)
            scatters[ex] = t
            y_free[k] = [t]
            idx_free[k] = [t]
            if ex + ZB < E:
                load_expert(ex + ZB, (t_work, t_work.value))

        out_rows = out.rearrange("b s d -> (b s) d")
        make_list(0)
        fill()
        gather(0)
        for _ in range(2):
            fill()
        make_list(1)
        gather(1)
        while filler:
            fill()
        b2_loaded = load("b2", b2_rep, b2.rearrange("e d -> (e d)").partition_broadcast(P), [tr_free[0]])
        hid_free[0], hid_free[1] = u_free[:], u_free[:]
        turned = turn_gathered(0)
        for ex in range(E):
            expert_up(ex, turned)
            if ex + 1 < E:
                turned = turn_gathered(ex + 1)
            expert_down(ex)
            if ex + 2 < E:
                make_list(ex + 2)
                gather(ex + 2)
        put("gpsimd", lambda e: e.nop(), [scatters[E - 1]])

        block = ctx.enter_context(nc.Block())

        @block.sync
        def _(eng):
            plan.run("sync", eng)

        @block.gpsimd
        def _(eng):
            plan.run("gpsimd", eng)

        @block.scalar
        def _(eng):
            plan.run("scalar", eng)

        @block.tensor
        def _(eng):
            plan.run("tensor", eng)

        @block.vector
        def _(eng):
            plan.run("vector", eng)


_INS = ['x', 'ctx_1024', 'mask_BxS2_ik0', 'L0_xattn_Ws', 'L0_xattn_W', 'L0_xattn_w', 'L0_xattn_b', 'L0_xattn_Wcw',
        'L0_xattn_bcw', 'L0_xattn_Wcb', 'L0_xattn_bcb', 'L0_ffn_gate', 'L0_ffn_W1', 'L0_ffn_b1', 'L0_ffn_W2',
        'L0_ffn_b2', 'L0_ffn_Ws1', 'L0_ffn_bs1', 'L0_ffn_Ws2', 'L0_ffn_bs2']


def kernel(**inputs):
    import numpy as _np
    import concourse.bacc as _bacc
    from concourse import mybir as _mybir
    from concourse.bass_utils import run_bass_kernel_spmd as _run

    nc = _bacc.Bacc("TRN2", target_bir_lowering=False, num_devices=1)
    arrays, args = {}, []
    for name in _INS:
        a = _np.ascontiguousarray(inputs[name])
        arrays[f"in_{name}_dram"] = a
        args.append(nc.dram_tensor(f"in_{name}_dram", a.shape, _mybir.dt.from_np(a.dtype), kind="ExternalInput").ap())
    shape = tuple(inputs['x'].shape)
    out = nc.dram_tensor("out_0_dram", shape, _mybir.dt.float32, kind="ExternalOutput").ap()
    xn2 = nc.dram_tensor("xn2_dram", (shape[0] * shape[1], shape[2]), _mybir.dt.float32, kind="Internal").ap()
    xattn_moe_kernel(nc, *args, out, xn2)
    r = _run(nc, [arrays], core_ids=[0])
    return r.results[0]["out_0_dram"]
```

```python
from contextlib import ExitStack

import concourse.bass as bass
from concourse import mybir

F32 = mybir.dt.float32
F32R = mybir.dt.float32r
I32 = mybir.dt.int32
U32 = mybir.dt.uint32
ALU = mybir.AluOpType
ACT = mybir.ActivationFunctionType
AX = mybir.AxisListType

P = 128
BANK = 512
EPS = 1e-5
NEG = 1e30
PAD = -3.0e38
CAP_FACTOR = 1.0
MIN_CAP = 8
RSQRT_MAGIC = 1597463007.0
FIRST_BIT = 29


class Signal:

    def __init__(self, sem):
        self.sem, self.value = sem, 0


class Plan:

    def __init__(self):
        self.queues = {name: [] for name in ("tensor", "vector", "scalar", "gpsimd", "sync")}

    def put(self, engine, emit, after=(), signal=None, by=1):
        self.queues[engine].append((emit, list(after), signal.sem if signal else None, by))
        if signal is None:
            return None
        signal.value += by
        return signal, signal.value

    def run(self, engine, eng):
        reached = {}
        for emit, after, sem, by in self.queues[engine]:
            for signal, value in after:
                if reached.get(id(signal), 0) < value:
                    eng.wait_ge(signal.sem, value)
                    reached[id(signal)] = value
            ins = emit(eng)
            if sem is not None:
                ins.then_inc(sem, by)


BASE = 16512
TOP = 229344


def xattn_moe_kernel(nc, x, ctx_rows, ctx_mask, Ws, W, w, b, Wcw, bcw, Wcb, bcb,
                     gate, W1, b1, W2, b2, Ws1, bs1, Ws2, bs2, out, xn2_dram):
    B, S, D = x.shape
    T = ctx_rows.shape[1]
    E, _, H = W1.shape
    C = D // P
    M = H // P
    TOK = BANK
    J = TOK // P
    UPB = S // TOK
    UNITS = B * UPB
    NTOK = B * S
    NT = NTOK // P
    CAP = max(MIN_CAP, int(CAP_FACTOR * NTOK / E))
    A = CAP // P
    G = 4
    I = -(-T // G)
    R = G * I
    BLOCKS = I
    ZB, XB, NB = 3, 6, 3
    JT = P // E
    NH = NT // JT
    HC = 4
    NL = 3
    assert D % P == 0 and CAP == TOK and I <= 32 and NT % JT == 0 and NH == 2 and UNITS % 2 == 0 and P % E == 0

    plan = Plan()
    put = plan.put

    with ExitStack() as ctx:
        cursor = [BASE]

        def sb(name, shape, dt=F32, at=None):
            n = 1
            for k in shape[1:]:
                n *= k
            where = cursor[0] if at is None else at
            if at is None:
                cursor[0] += -(-n * 4 // 32) * 32
            return nc.alloc_sbuf_tensor_at(name, shape, dt, offset=where)

        def signal(name):
            return Signal(ctx.enter_context(nc.semaphore(name)))

        gate_sb = sb("gate_sb", [P, C, E])
        gate_s = sb("gate_s", [P, 2, C, E], F32R)
        bs2_rep = sb("bs2_rep", [P, D])
        mask_rep = sb("mask_rep", [P, B, R])
        cww_rep = sb("cww_rep", [P, B, R])
        cwb_rep = sb("cwb_rep", [P, B, R])
        txt_bias = sb("txt_bias", [P, C, B * T])
        window = sb("window", [P, C, 63])
        ident = sb("ident", [P, P])
        ones = sb("ones", [P, P])
        same_expert = sb("same_expert", [P, P])
        earlier_tile = sb("earlier_tile", [P, P])
        expert_of = sb("expert_of", [P, E])
        fold = sb("fold", [P, 32])
        iota_slot = sb("iota_slot", [P, P])
        iota_a = sb("iota_a", [P, A])
        tok_id = sb("tok_id", [P, NT])
        NV = M * E + M + 4 * C
        vec_rows = sb("vec_rows", [NV, P])
        vec = sb("vec", [P, NV])
        bc = sb("bc", [P, 2])
        ln_scratch = [(sb(f"stats{i}", [P, J, 6]), sb(f"mv{i}", [P, J, 2]), sb(f"ve{i}", [P, J]),
                       sb(f"ry{i}", [P, J]), sb(f"ra{i}", [P, J])) for i in range(2)]
        sm = sb("sm", [P, 8, J])
        wb = sb("wb", [P, 2, J])
        lg = sb("lg", [P, J, E])
        probs = sb("probs", [P, NT, E])
        pt = sb("pt", [P, NH * P])
        eq = sb("eq", [P, NH * P])
        gt = sb("gt", [P, NH * P])
        scan = sb("scan", [P, NH * P])
        cur = sb("cur", [P, 4], I32)
        okbit = sb("okbit", [P, 2], I32)
        cnt = sb("cnt", [P, 8])
        off = sb("off", [P, NH])
        picked = sb("picked", [P, P])
        idx = sb("idx", [P, NL, A], I32)
        score = sb("score", [P, NL, A])

        first = cursor[0]
        z = sb("z", [P, ZB, G * C * TOK])
        feat = sb("feat", [P, 2, C, TOK])
        xn = sb("xn", [P, NB, J, D])
        tr_x = sb("tr_x", [P, C, TOK])
        rho_sb = sb("rho_sb", [P, TOK])
        att = sb("att", [P, J, R])
        att_tmp = sb("att_tmp", [P, J, R])
        w_sb = sb("w_sb", [P, C, D])
        ws_sb = sb("ws_sb", [P, C, D])
        early_end = cursor[0]
        tr_at = cursor[0]
        tr = sb("tr", [P, 2, 2, C, TOK], F32R)
        ws1_at = cursor[0]
        ws1_s = sb("ws1_s", [P, 2, C, H], F32R)
        ws2_sb = sb("ws2_sb", [P, M, D])
        x_at = cursor[0]
        x_ring = sb("x_ring", [P, XB, J, D])
        u_at = cursor[0]
        u = sb("u", [P, 2, M, TOK])
        assert cursor[0] <= TOP, cursor[0]

        cursor[0] = first
        w1_s = [sb("w1_s0", [P, 2, C, H], F32R)]
        w2_s = [sb("w2_s0", [P, 2, M, D], F32R)]
        w1_raw = sb("w1_raw", [P, C, H])
        w2_raw = sb("w2_raw", [P, M, D])
        onehot = sb("onehot", [P, NT, P])
        pick = sb("pick", [P, NT, 32])
        slot_i = sb("slot_i", [P, NT * E], I32)
        slot_c = sb("slot_c", [P, NT, E])
        slot_a = sb("slot_a", [P, NT, E])
        assert cursor[0] <= early_end, (cursor[0], early_end)
        xg_s = sb("xg_s", [P, 2, 2, C, TOK], F32R, at=tr_at)
        w1_s.append(sb("w1_s1", [P, 2, C, H], F32R, at=ws1_at))
        w2_s.append(sb("w2_s1", [P, 2, M, D], F32R, at=ws1_at + 2 * C * H * 4))
        unit_bytes = J * D * 4
        assert ws1_at + 2 * (C * H + M * D) * 4 <= x_at + 2 * unit_bytes
        assert [v % XB for v in (UNITS - 2, UNITS - 1)] == [0, 1]
        xg = sb("xg", [P, 2, A, D], at=x_at + 2 * unit_bytes)
        b2_rep = sb("b2_rep", [P, E, D], at=x_at + 4 * unit_bytes)
        cursor[0] = u_at
        hid = sb("hid", [P, HC, TOK])
        hid_s = sb("hid_s", [P, HC, 2, TOK], F32R)
        y = sb("y", [P, 2, A, D])
        assert cursor[0] <= TOP
        ctx_sb = z[0:T, 2, 0:B * D].rearrange("p (b d) -> p b d", b=B)
        txt_t = z[:, 2, B * D:B * D + C * B * T].rearrange("p (c n) -> p c n", c=C)
        wide = z[:, 2, 2048:2048 + 2 * C * P].rearrange("p (v c m) -> p v c m", v=2, c=C)
        row = z[:, 2, 2560:2560 + 3 * B * R].rearrange("p (v b r) -> p v b r", v=3, b=B)
        mask_i = z[:, 1, 0:B * T].bitcast(I32)
        ws1_raw = u[:, 1, 0:C * H // TOK, :].rearrange("p m s -> p (m s)").rearrange("p (c h) -> p c h", c=C)

        banks = [ctx.enter_context(nc.psum_tensor(f"bank{i}", [P, BANK], F32)) for i in range(8)]
        RHO, UP, DOWN, MISC = (0, 1), (2, 3), (4, 5), (6, 7)
        released = {i: [] for i in range(8)}

        loaded = {}

        def load(name, dst, src, after=()):
            s = signal(f"ld_{name}")
            loaded[name] = put("sync", lambda e: e.dma_start(dst, src), after, s, 16)
            return loaded[name]

        pool_const = signal("pool_const")
        pool_add = signal("pool_add")
        pool_split = signal("pool_split")
        v_chain = signal("v_chain")
        v_add = signal("v_add")
        a_tanh = signal("a_tanh")
        a_small = signal("a_small")
        a_gelu = signal("a_gelu")
        a_split = signal("a_split")
        t_rho = signal("t_rho")
        t_work = signal("t_work")
        stored = [signal(f"stored{i}") for i in range(UNITS)]
        xn2_stored = [signal(f"xn2_stored{i}") for i in range(UNITS)]
        gathered = [signal(f"gathered{i}") for i in range(2)]
        scattered = signal("scattered")

        def vec_op(emit, *after):
            return put("vector", emit, after, v_chain)

        def pe(emit, *after):
            return put("tensor", emit, after, t_work)

        def split_matmul(e, dst, lhs, rhs, start, stop, terms=((1, 0), (0, 1), (0, 0))):
            for n, (a, c) in enumerate(terms):
                ins = e.matmul(dst, lhs(a), rhs(c), start=start and n == 0, stop=stop and n == len(terms) - 1)
            return ins

        def load_x(v, after=()):
            xr = x[v // UPB, (v % UPB) * TOK:(v % UPB + 1) * TOK, :].rearrange("(j p) d -> p j d", p=P)
            return load(f"x{v}", x_ring[:, v % XB], xr, after)

        load_x(0)
        load("w", w_sb[:], W.rearrange("(c p) d -> p c d", p=P))
        load("ctx", ctx_sb, ctx_rows.rearrange("b t d -> t b d"))
        load("ws", ws_sb[:], Ws.rearrange("(c p) d -> p c d", p=P))
        vec_sources = [("b1", b1.rearrange("e (m p) -> (e m) p", p=P)),
                       ("bs1", bs1.rearrange("(m p) -> m p", p=P)),
                       ("b", b.rearrange("a (c p) -> (a c) p", p=P)),
                       ("Wcw", Wcw.rearrange("a (c p) -> (a c) p", p=P)),
                       ("Wcb", Wcb.rearrange("a (c p) -> (a c) p", p=P)),
                       ("w_col", w.rearrange("(c p) a -> (c a) p", p=P))]
        at, col = 0, {}
        for name, src in vec_sources:
            n = src.shape[0]
            load("v_" + name, vec_rows[at:at + n, :], src)
            col[name] = at
            at += n
        assert at == NV
        load("mask", mask_i, ctx_mask.rearrange("b t -> (b t)").partition_broadcast(P))
        load("bcw", bc[:, 0:1], bcw.partition_broadcast(P))
        load("bcb", bc[:, 1:2], bcb.partition_broadcast(P))
        load("gate", gate_sb[:], gate.rearrange("(c p) e -> p c e", p=P))
        load("bs2", bs2_rep[:], bs2.partition_broadcast(P))
        load_x(1)
        load("ws1", ws1_raw, Ws1.rearrange("(c p) h -> p c h", p=P))
        load("ws2", ws2_sb[:], Ws2.rearrange("(m p) d -> p m d", p=P))
        for v in range(2, XB):
            load_x(v)

        def const(emit, *after):
            return put("gpsimd", emit, after, pool_const)

        c0 = const(lambda e: e.memset(ident[:], 0.0))
        ident_ok = const(lambda e: e.affine_select(out=ident[:], in_=ident[:], compare_op=ALU.not_equal, fill=1.0,
                                                   base=0, pattern=[[-1, P]], channel_multiplier=1), c0)
        ones_ok = const(lambda e: e.memset(ones[:], 1.0))
        row_ok = const(lambda e: e.memset(row, 0.0))
        win0 = const(lambda e: e.memset(window[:], 0.0))
        const(lambda e: e.iota(iota_slot[:], [[1, P]], base=0, channel_multiplier=0,
                               allow_small_or_imprecise_dtypes=True))
        const(lambda e: e.iota(iota_a[:], [[1, A]], base=0, channel_multiplier=0,
                               allow_small_or_imprecise_dtypes=True))
        iota_ok = const(lambda e: e.iota(tok_id[:], [[P, NT]], base=0, channel_multiplier=1,
                                         allow_small_or_imprecise_dtypes=True))

        def layer_norm_stats(src, scratch, *after):
            stats, mv, ve, ry, ra = scratch
            for j in range(J):
                t = vec_op(lambda e, j=j: e.bn_stats(stats[:, j, :], src[:, j, :]), *after)
            for j in range(J):
                t2 = vec_op(lambda e, j=j: e.bn_aggr(mv[:, j, :], stats[:, j, :]), t)
            t = vec_op(lambda e: e.tensor_scalar(ve[:], mv[:, :, 1], EPS, None, ALU.add), t2)
            t = vec_op(lambda e: e.tensor_scalar(ry[:].bitcast(I32), ve[:].bitcast(I32), 1, None,
                                                 ALU.logical_shift_right), t)
            t = vec_op(lambda e: e.tensor_scalar(ry[:].bitcast(I32), ry[:].bitcast(I32), -1.0, RSQRT_MAGIC,
                                                 ALU.mult, ALU.add), t)
            for _ in range(3):
                t = vec_op(lambda e: e.scalar_tensor_tensor(out=ra[:], in0=ry[:], scalar=-0.5, in1=ry[:],
                                                            op0=ALU.mult, op1=ALU.mult), t)
                t = vec_op(lambda e: e.tensor_tensor(ra[:], ra[:], ve[:], ALU.mult), t)
                t = vec_op(lambda e: e.scalar_tensor_tensor(out=ry[:], in0=ra[:], scalar=1.5, in1=ry[:],
                                                            op0=ALU.add, op1=ALU.mult), t)
            return t

        def normalise(src, dst, scratch, *after):
            _, mv, _, ry, _ = scratch
            for j in range(J):
                t = vec_op(lambda e, j=j: e.tensor_scalar(dst[:, j, :], src[:, j, :], mv[:, j, 0:1], ry[:, j:j + 1],
                                                          ALU.subtract, ALU.mult), *after)
            return t

        def transposes(bank, src, c, *after):
            def four(e):
                for j in range(J):
                    ins = e.transpose(banks[bank][:, j * P:(j + 1) * P], src[:, j, c * P:(c + 1) * P], ident[:])
                return ins
            return pe(four, ident_ok, *after, *released[bank])

        feat_ready, tr_ready, x2_ready, probs_ready, rho_last, up_done = {}, {}, {}, {}, {}, {}
        feat_free = {0: [], 1: []}
        xn_free = {n: [] for n in range(NB)}
        tr_free = {0: [], 1: []}
        tr_x_free, rho_sb_free, att_free = [], [], []
        u_free = {0: [], 1: []}

        def pre_steps(v):
            src, dst = x_ring[:, v % XB], xn[:, v % NB]
            hold = {}

            def stats():
                hold["t"] = layer_norm_stats(src, ln_scratch[0], loaded[f"x{v}"])

            def apply():
                hold["t"] = normalise(src, dst, ln_scratch[0], hold["t"], *xn_free[v % NB])

            def turn():
                hold["t"] = [transposes(MISC[c], dst, c, hold["t"]) for c in range(C)]

            def turned():
                for c in range(C):
                    t = vec_op(lambda e, c=c: e.tensor_copy(tr_x[:, c, :], banks[MISC[c]][:]), hold["t"][c],
                               *tr_x_free)
                    released[MISC[c]] = [t]
                hold["tr"] = t
                project(0)

            def project(co):
                def mm(e):
                    for c in range(C):
                        ins = e.matmul(banks[MISC[co]][:], w_sb[:, c, co * P:(co + 1) * P], tr_x[:, c, :],
                                       start=c == 0, stop=c == C - 1)
                    return ins
                hold[co] = pe(mm, hold["tr"], loaded["w"], *released[MISC[co]])

            def projected(co):
                t = vec_op(lambda e: e.tensor_copy(feat[:, v % 2, co, :], banks[MISC[co]][:]), hold[co],
                           *feat_free[v % 2])
                released[MISC[co]] = [t]
                feat_ready[v] = t

            def middle():
                project(1)
                projected(0)

            def end():
                tr_x_free[:] = [hold[1]]
                projected(1)

            return [stats, apply, turn, turned, middle, end]

        def tail_steps(v):
            xs, ns = x_ring[:, v % XB], xn[:, v % NB]
            batch, rho_bank = v // UPB, RHO[v % 2]
            hold = {}

            def evacuate():
                hold["t"] = vec_op(lambda e: e.tensor_copy(rho_sb[:], banks[rho_bank][:]), rho_last[v], *rho_sb_free)
                released[rho_bank] = [hold["t"]]

            def to_tokens():
                n = MISC[0]

                def four(e):
                    for j in range(J):
                        ins = e.transpose(banks[n][:, j * P:(j + 1) * P], rho_sb[:, j * P:(j + 1) * P], ident[:])
                    return ins
                hold["t"] = pe(four, hold["t"], ident_ok, *released[n])
                rho_sb_free[:] = [hold["t"]]

            def shift():
                n = MISC[0]
                rt = banks[n][:].rearrange("p (j g i) -> p j g i", j=J, g=G)
                for j in range(J):
                    t = vec_op(lambda e, j=j: e.tensor_tensor(
                        att[:, j, :].rearrange("p (g i) -> p g i", g=G), rt[:, j, :, 0:I],
                        mask_rep[:, batch, :].rearrange("p (g i) -> p g i", g=G), ALU.add), hold["t"])
                released[n] = [t]
                t = vec_op(lambda e: e.tensor_reduce(sm[:, 0, :], att[:], AX.X, ALU.max), t)
                hold["t"] = vec_op(lambda e: e.tensor_tensor(
                    att[:], att[:], sm[:, 0, :].unsqueeze(2).broadcast_to([P, J, R]), ALU.subtract), t)

            def exp():
                hold["t"] = put("scalar", lambda e: e.activation(att[:], att[:], ACT.Exp), [hold["t"]], a_small)

            def weigh():
                t0 = hold["t"]
                t = vec_op(lambda e: e.tensor_reduce(sm[:, 1, :], att[:], AX.X, ALU.add), t0)
                vec_op(lambda e: e.reciprocal(sm[:, 2, :], sm[:, 1, :]), t)
                for n, rep in enumerate((cww_rep, cwb_rep)):
                    t = vec_op(lambda e, rep=rep: e.tensor_tensor(
                        att_tmp[:], att[:], rep[:, batch, :].unsqueeze(1).broadcast_to([P, J, R]), ALU.mult), t)
                    t = vec_op(lambda e, n=n: e.tensor_reduce(wb[:, n, :], att_tmp[:], AX.X, ALU.add), t)
                t = vec_op(lambda e: e.tensor_tensor(wb[:], wb[:], sm[:, 2, :].unsqueeze(1).broadcast_to([P, 2, J]),
                                                     ALU.mult), t)
                hold["t"] = vec_op(lambda e: e.tensor_tensor(wb[:], wb[:], bc[:].unsqueeze(2).broadcast_to([P, 2, J]),
                                                             ALU.add), t, loaded["bcw"], loaded["bcb"])

            def gates():
                hold["t"] = put("scalar", lambda e: e.activation(wb[:], wb[:], ACT.Tanh), [hold["t"]], a_small)

            def residual():
                for j in range(J):
                    t = vec_op(lambda e, j=j: e.tensor_scalar(ns[:, j, :], ns[:, j, :], wb[:, 0, j:j + 1],
                                                              wb[:, 1, j:j + 1], ALU.mult, ALU.add), hold["t"])
                t = vec_op(lambda e: e.tensor_tensor(xs, xs, ns, ALU.add), t)
                hold["t"] = layer_norm_stats(xs, ln_scratch[1], t)

            def apply():
                t = normalise(xs, ns, ln_scratch[1], hold["t"])
                hold["t"] = t
                x2_ready[v] = vec_op(lambda e: e.tensor_tensor(
                    xs, xs, bs2_rep[:].unsqueeze(1).broadcast_to([P, J, D]), ALU.add), t, loaded["bs2"])
                hold["store"] = put("sync", lambda e: e.dma_start(
                    xn2_dram[v * TOK:(v + 1) * TOK, :].rearrange("(j p) d -> p j d", p=P), ns),
                    [t], xn2_stored[v], 16)

            def turn():
                hold["t"] = [transposes(MISC[c], ns, c, hold["t"]) for c in range(C)]
                xn_free[v % NB] = [hold["t"][-1], hold["store"]]

            def turned():
                for c in range(C):
                    src = banks[MISC[c]]
                    t = vec_op(lambda e, c=c, src=src: e.tensor_copy(tr[:, v % 2, 0, c, :], src[:]), hold["t"][c],
                               *tr_free[v % 2])
                    t = vec_op(lambda e, c=c, src=src: e.tensor_tensor(
                        tr[:, v % 2, 1, c, :], src[:], tr[:, v % 2, 0, c, :].bitcast(F32), ALU.subtract), t)
                    released[MISC[c]] = [t]
                tr_ready[v] = t

            def logits():
                n = MISC[0]

                def mm(e):
                    for j in range(J):
                        for c in range(C):
                            ins = split_matmul(e, banks[n][:, j * E:(j + 1) * E],
                                               lambda i: tr[:, v % 2, i, c, j * P:(j + 1) * P],
                                               lambda i: gate_s[:, i, c, :], c == 0, c == C - 1)
                    return ins
                hold["t"] = pe(mm, tr_ready[v], gate_ok[0], *released[n])
                tr_free[v % 2] = [hold["t"]]

            def shift_logits():
                n = MISC[0]
                lp = banks[n][:, 0:J * E].rearrange("p (j e) -> p j e", j=J)
                t = vec_op(lambda e: e.tensor_reduce(sm[:, 3, :], lp, AX.X, ALU.max), hold["t"])
                hold["t"] = vec_op(lambda e: e.tensor_tensor(
                    lg[:], lp, sm[:, 3, :].unsqueeze(2).broadcast_to([P, J, E]), ALU.subtract), t)
                released[n] = [hold["t"]]

            def exp_logits():
                hold["t"] = put("scalar", lambda e: e.activation(lg[:], lg[:], ACT.Exp), [hold["t"]], a_small)

            def router():
                t = vec_op(lambda e: e.tensor_reduce(sm[:, 4, :], lg[:], AX.X, ALU.add), hold["t"])
                t = vec_op(lambda e: e.reciprocal(sm[:, 5, :], sm[:, 4, :]), t)
                probs_ready[v] = vec_op(lambda e: e.tensor_tensor(
                    probs[:, v * J:(v + 1) * J, :], lg[:], sm[:, 5, :].unsqueeze(2).broadcast_to([P, J, E]),
                    ALU.mult), t)

            return [evacuate, to_tokens, shift, exp, weigh, gates, residual, apply, turn, turned, logits,
                    shift_logits, exp_logits, router]

        def up_product(v, m, bank, chunks, after):
            def mm(e):
                for c in chunks:
                    ins = split_matmul(e, banks[bank][:], lambda i: ws1_s[:, i, c, m * P:(m + 1) * P],
                                       lambda i: tr[:, v % 2, i, c, :], c == 0, c == C - 1)
                return ins
            return pe(mm, *after)

        def up_steps(v):
            hold = {}

            def up(m):
                if m < M:
                    bank = UP[m % 2]
                    hold[m] = up_product(v, m, bank, range(C), [tr_ready[v], ws1_ok[0], *released[bank]])
                    tr_free[v % 2] = [hold[m]]
                if m > 0:
                    bank = UP[(m - 1) % 2]
                    up_done[v] = vec_op(lambda e: e.tensor_scalar(
                        u[:, v % 2, m - 1, :], banks[bank][:], vec[:, col["bs1"] + m - 1:col["bs1"] + m], None,
                        ALU.add), hold[m - 1], vec_ready[0], *u_free[v % 2])
                    released[bank] = [up_done[v]]
            return [lambda m=m: up(m) for m in range(M + 1)]

        gelu_done = {}

        def gelu(v):
            part = u[:, v % 2]
            gelu_done[v] = put("scalar", lambda e: e.activation(part, part, ACT.Gelu_apprx_tanh), [up_done[v]], a_gelu)

        def down_product(v, j, bank, chunks, after):
            def mm(e):
                for m in chunks:
                    ins = e.matmul(banks[bank][:, 0:D], u[:, v % 2, m, j * P:(j + 1) * P], ws2_sb[:, m, :],
                                   start=m == 0, stop=m == M - 1)
                return ins
            return pe(mm, *after)

        def down_end(v, j, bank, t):
            xs = x_ring[:, v % XB]
            done = vec_op(lambda e: e.tensor_tensor(xs[:, j, :], banks[bank][:, 0:D], xs[:, j, :], ALU.add), t,
                          x2_ready[v])
            released[bank] = [done]
            if j == J - 1:
                u_free[v % 2] = [t]
                rows = out[v // UPB, (v % UPB) * TOK:(v % UPB + 1) * TOK, :]
                s = put("sync", lambda e: e.dma_start(rows.rearrange("(j p) d -> p j d", p=P), xs), [done],
                        stored[v], 16)
                if v + XB < UNITS:
                    load_x(v + XB, [s])

        def down_steps(v):
            hold = {}

            def down(j, half):
                bank = DOWN[j % 2]
                if half == 0 and j > 0:
                    down_end(v, j - 1, DOWN[(j - 1) % 2], hold["t"])
                if j < J:
                    hold["t"] = down_product(v, j, bank, range(half * M // 2, (half + 1) * M // 2),
                                             [gelu_done[v], loaded["ws2"], *released[bank]])
            return [lambda j=j, half=half: down(j, half) for j in range(J) for half in range(2)] + \
                [lambda: down(J, 0)]

        for step in pre_steps(0):
            step()

        t = pe(lambda e: e.transpose(banks[2][:, 0:NV], vec_rows[:], ident[0:NV, 0:NV]), ident_ok,
               *[loaded["v_" + name] for name, _ in vec_sources])
        vec_ready = [vec_op(lambda e: e.tensor_copy(vec[:], banks[2][:, 0:NV]), t)]
        released[2] = vec_ready[:]
        window_ready = [vec_op(lambda e: e.tensor_copy(window[:, :, 31], vec[:, col["w_col"]:col["w_col"] + C]),
                               vec_ready[0], win0)]

        def ctx_transposes(e, c):
            for bb in range(B):
                ins = e.transpose(banks[4 + c][:, bb * T:(bb + 1) * T], ctx_sb[:, bb, c * P:(c + 1) * P],
                                  ident[0:T, 0:T])
            return ins
        for c in range(C):
            t = pe(lambda e, c=c: ctx_transposes(e, c), loaded["ctx"], ident_ok)
            t = vec_op(lambda e, c=c: e.tensor_copy(txt_t[:, c, :], banks[4 + c][:, 0:B * T]), t)
            released[4 + c] = [t]
        txt_t_ready = t
        for co in range(C):
            def mm(e, co=co):
                for c in range(C):
                    ins = e.matmul(banks[2 + co][:, 0:B * T], ws_sb[:, c, co * P:(co + 1) * P], txt_t[:, c, :],
                                   start=c == 0, stop=c == C - 1)
                return ins
            t = pe(mm, txt_t_ready, loaded["ws"], *released[2 + co])
            t = vec_op(lambda e, co=co: e.tensor_scalar(txt_bias[:, co, :], banks[2 + co][:, 0:B * T],
                                                        vec[:, col["b"] + co:col["b"] + co + 1], None, ALU.add), t,
                       vec_ready[0])
            released[2 + co] = [t]
        txt_ready = [t]

        z_free = {n: [] for n in range(ZB)}
        added, tanhed = {}, {}
        LAST = UNITS * BLOCKS

        def block_of(n):
            v, k = n // BLOCKS, n % BLOCKS
            return v, k, [t for t in range(G * k, G * k + G) if t < T]

        def add_block(n):
            v, k, rows = block_of(n)
            zb = z[:, n % ZB, :].rearrange("p (r c s) -> p r c s", r=G, c=C)
            done = {}
            for r, t in enumerate(rows):
                for c in range(C):
                    pool = r == G - 1
                    emit = lambda e, r=r, t=t, c=c, pool=pool: e.tensor_scalar(
                        zb[:, r, c, :], feat[:, v % 2, c, :], txt_bias[:, c, v // UPB * T + t:v // UPB * T + t + 1],
                        1.0 if pool else None, ALU.add, *([ALU.mult] if pool else []))
                    after = [feat_ready[v], txt_ready[0], *z_free[n % ZB]]
                    if pool:
                        done["pool"] = put("gpsimd", emit, after, pool_add)
                    else:
                        done["vector"] = put("vector", emit, after, v_add)
            added[n] = list(done.values())
            if k == BLOCKS - 1:
                feat_free[v % 2] = added[n] + added[n - 1]

        def tanh_block(n):
            _, _, rows = block_of(n)
            part = z[:, n % ZB, 0:len(rows) * C * TOK]
            tanhed[n] = put("scalar", lambda e: e.activation(part, part, ACT.Tanh), added[n], a_tanh)

        def rho_block(n):
            v, k, rows = block_of(n)
            zb = z[:, n % ZB, :].rearrange("p (r c s) -> p r c s", r=G, c=C)
            bank = RHO[v % 2]

            def mm(e):
                for c in range(C):
                    for r, t in enumerate(rows):
                        ins = e.matmul(banks[bank][32 * r:32 * r + 32, :], window[:, c, 31 - k:63 - k],
                                       zb[:, r, c, :], start=(c == 0 and k == 0), stop=(c == C - 1 and t + G >= T))
                return ins

            tok = put("tensor", mm, [tanhed[n], window_ready[0], *(released[bank] if k == 0 else [])], t_rho)
            z_free[n % ZB] = [tok]
            rho_last[v] = tok

        add_block(0)
        tanh_block(0)

        for v, name in enumerate(("Wcw", "Wcb")):
            for c in range(C):
                t = vec_op(lambda e, v=v, c=c, name=name: e.tensor_scalar(
                    wide[:, v, c, :], ones[:], vec[:, col[name] + c:col[name] + c + 1], None, ALU.mult),
                    vec_ready[0], ones_ok)
        wide_ready = t
        t = vec_op(lambda e: e.tensor_scalar(row[:, 0, :, 0:T], mask_i.rearrange("p (b t) -> p b t", b=B), 1.0, NEG,
                                             ALU.subtract, ALU.mult), loaded["mask"], row_ok)
        z_free[1] = [t]
        if R > T:
            vec_op(lambda e: e.memset(row[:, 0, :, T:R], PAD), row_ok)
        for v in range(2):
            def mm(e, v=v):
                for c in range(C):
                    ins = e.matmul(banks[DOWN[v]][:, 0:B * T], wide[:, v, c, :], txt_t[:, c, :],
                                   start=c == 0, stop=c == C - 1)
                return ins
            t = pe(mm, wide_ready, txt_t_ready, *released[DOWN[v]])
            t = vec_op(lambda e, v=v: e.tensor_copy(row[:, 1 + v, :, 0:T],
                                                    banks[DOWN[v]][:, 0:B * T].rearrange("p (b t) -> p b t", b=B)),
                       t, row_ok)
            released[DOWN[v]] = [t]
        for v, rep in enumerate((mask_rep, cww_rep, cwb_rep)):
            t2 = vec_op(lambda e, v=v, rep=rep: e.tensor_copy(
                rep[:].rearrange("p b (g i) -> p b g i", g=G), row[:, v, :, :].rearrange("p b (i g) -> p b g i", g=G)),
                t)
        z_free[2] = [t2]
        add_block(1)

        t = vec_op(lambda e: e.tensor_copy(gate_s[:, 0], gate_sb[:]), loaded["gate"])
        gate_ok = [vec_op(lambda e: e.tensor_tensor(gate_s[:, 1], gate_sb[:], gate_s[:, 0].bitcast(F32),
                                                    ALU.subtract), t)]
        t = vec_op(lambda e: e.tensor_reduce(expert_of[:], ident[:].rearrange("p (t e) -> p e t", e=E), AX.X, ALU.add),
                   ident_ok)
        vec_op(lambda e: e.tensor_reduce(fold[:], ident[:].rearrange("p (g r) -> p r g", r=32), AX.X, ALU.add),
               ident_ok)
        router_consts = vec_op(lambda e: e.tensor_copy(same_expert[:].rearrange("p (t e) -> p t e", e=E),
                                                       expert_of[:].unsqueeze(1).broadcast_to([P, JT, E])), t)
        earlier_ok = const(lambda e: e.affine_select(out=earlier_tile[:], in_=same_expert[:], compare_op=ALU.is_gt,
                                                     fill=0.0, base=0, pattern=[[1, P]], channel_multiplier=-1),
                           router_consts)

        ws1_ok = []

        def split_ws1(c):
            t = vec_op(lambda e: e.tensor_copy(ws1_s[:, 0, c, :], ws1_raw[:, c, :]), loaded["ws1"])
            ws1_ok[:] = [vec_op(lambda e: e.tensor_tensor(ws1_s[:, 1, c, :], ws1_raw[:, c, :],
                                                          ws1_s[:, 0, c, :].bitcast(F32), ALU.subtract), t)]
            u_free[1] = ws1_ok[:]

        for n in range(LAST):
            v, k, _ = block_of(n)
            if k == 0:
                slots = [[] for _ in range(BLOCKS)]

                def at_slots(first_slot, steps):
                    for i, step in enumerate(steps):
                        slots[min(first_slot + i, BLOCKS - 1)].append(step)

                if v == 0:
                    at_slots(10, [lambda c=c: split_ws1(c) for c in range(C)])
                if v > 0:
                    at_slots(0, tail_steps(v - 1))
                if v + 1 < UNITS:
                    at_slots(2, pre_steps(v + 1))
                if v >= 2 and v % 2 == 0:
                    at_slots(0, up_steps(v - 2))
                    at_slots(10, up_steps(v - 1))
                if v >= 3 and v % 2 == 1:
                    at_slots(0, [lambda: gelu(v - 3)])
                    at_slots(1, [lambda: gelu(v - 2)])
                    at_slots(1, down_steps(v - 3))
                    at_slots(10, down_steps(v - 2))
            if n + 2 < LAST:
                add_block(n + 2)
            if n + 1 < LAST:
                tanh_block(n + 1)
            rho_block(n)
            for step in slots[k]:
                step()

        va, vb = UNITS - 2, UNITS - 1
        ups = []

        def up_identity(m):
            bank = UP[m % 2]
            t = up_product(va, m, bank, range(C), [tr_ready[va], ws1_ok[0], *released[bank]])
            up_done[va] = put("scalar", lambda e: e.activation(
                u[:, va % 2, m, :], banks[bank][:], ACT.Identity, bias=vec[:, col["bs1"] + m:col["bs1"] + m + 1]),
                [t, vec_ready[0], *u_free[va % 2]], a_gelu)
            released[bank] = [up_done[va]]
            tr_free[va % 2] = [t]

        m = 0
        for i, step in enumerate(tail_steps(vb)):
            step()
            if m < M and i not in (2, 4):
                up_identity(m)
                m += 1
        assert m == M
        gelu(va)
        early_free = [probs_ready[vb], tanhed[LAST - 1], rho_last[vb], tr_ready[vb], (stored_xn2 := (xn2_stored[vb], 16))]

        w_free = {0: list(early_free), 1: []}
        w_ready = {}
        raw_free = {"w1": list(early_free), "w2": list(early_free)}

        def load_expert(ex):
            load(f"w1_{ex}", w1_raw[:], W1[ex].rearrange("(c p) h -> p c h", p=P), raw_free["w1"])
            load(f"w2_{ex}", w2_raw[:], W2[ex].rearrange("(m p) d -> p m d", p=P), raw_free["w2"])

        def split_expert(ex):
            k = ex % 2
            for name, raw, parts in (("w1", w1_raw, w1_s[k]), ("w2", w2_raw, w2_s[k])):
                t = put("scalar", lambda e, raw=raw, parts=parts: e.activation(parts[:, 0], raw[:], ACT.Copy),
                        [loaded[f"{name}_{ex}"], *w_free[k]], a_split)
                t = put("gpsimd", lambda e, raw=raw, parts=parts: e.tensor_tensor(
                    parts[:, 1], raw[:], parts[:, 0].bitcast(F32), ALU.subtract), [t], pool_split)
                raw_free[name] = [t]
                w_ready[name, ex] = t

        load_expert(0)
        split_expert(0)
        load_expert(1)

        filler = []
        hold = {}
        for m in range(M):
            def piece(m=m, c=None):
                bank = UP[m % 2]
                t = up_product(vb, m, bank, [c], [tr_ready[vb], *released[bank]])
                if c == C - 1:
                    gelu_done[vb] = put("scalar", lambda e: e.activation(
                        u[:, vb % 2, m, :], banks[bank][:], ACT.Gelu_apprx_tanh,
                        bias=vec[:, col["bs1"] + m:col["bs1"] + m + 1]), [t, *u_free[vb % 2]], a_gelu)
                    released[bank] = [gelu_done[vb]]
                    tr_free[vb % 2] = [t]
            filler += [lambda m=m, c=c, piece=piece: piece(m, c) for c in range(C)]
        for v in (va, vb):
            for j in range(J):
                def piece(q, v=v, j=j):
                    bank = DOWN[j % 2]
                    t = down_product(v, j, bank, range(2 * q, 2 * q + 2),
                                     [gelu_done[v], *(released[bank] if q == 0 else [])])
                    if q == M // 2 - 1:
                        down_end(v, j, bank, t)
                filler += [lambda q=q, piece=piece: piece(q) for q in range(M // 2)]

        def fill(n=1):
            for _ in range(n):
                if filler:
                    filler.pop(0)()

        for hf in range(NH):
            n = MISC[hf]
            t = pe(lambda e, hf=hf, n=n: e.transpose(
                banks[n][:, 0:P], probs[:, hf * JT:(hf + 1) * JT, :].rearrange("p t e -> p (t e)"), ident[:]),
                probs_ready[vb], *released[n])
            t = vec_op(lambda e, hf=hf, n=n: e.tensor_copy(pt[:, hf * P:(hf + 1) * P], banks[n][:, 0:P]), t)
            released[n] = [t]
        pt_ready = t
        cur_i, cand_i = cur[:, 0:1], cur[:, 1:2]
        vec_op(lambda e: e.memset(cur_i, 0))
        cand_ready = vec_op(lambda e: e.memset(cand_i, 1 << FIRST_BIT))
        TOTAL = RHO[0]
        tot_ps = banks[TOTAL]
        for bit in range(FIRST_BIT, -1, -1):
            t = vec_op(lambda e: e.tensor_scalar(gt[:], pt[:], cand_i.bitcast(F32), None, ALU.is_ge, ALU.add,
                                                 accum_out=cnt[:, 0:1]), cand_ready, pt_ready)
            t = pe(lambda e: e.matmul(tot_ps[:, 0:1], same_expert[:], cnt[:, 0:1], start=True, stop=True),
                   t, router_consts, *released[TOTAL])
            fill()
            t = vec_op(lambda e, bit=bit: e.tensor_scalar(okbit[:, 0:1], tot_ps[:, 0:1], float(CAP), float(1 << bit),
                                                          ALU.is_ge, ALU.mult), t)
            released[TOTAL] = [t]
            if bit:
                cand_ready = vec_op(lambda e, bit=bit: e.scalar_tensor_tensor(
                    out=cand_i, in0=okbit[:, 0:1], scalar=1 << (bit - 1), in1=cur_i, op0=ALU.bitwise_or,
                    op1=ALU.bitwise_or), t)
            cur_ready = vec_op(lambda e: e.tensor_tensor(cur_i, okbit[:, 0:1], cur_i, ALU.bitwise_or), t, cand_ready)

        thr = cur_i.bitcast(F32)
        t_above = vec_op(lambda e: e.tensor_scalar(gt[:], pt[:], thr, None, ALU.is_gt, ALU.add,
                                                   accum_out=cnt[:, 0:1]), cur_ready)
        t = pe(lambda e: e.matmul(tot_ps[:, 0:1], same_expert[:], cnt[:, 0:1], start=True, stop=True), t_above,
               *released[TOTAL])
        fill()
        t_eq = vec_op(lambda e: e.tensor_scalar(eq[:], pt[:], thr, None, ALU.is_equal), t_above)
        left = vec_op(lambda e: e.tensor_scalar(cnt[:, 1:2], tot_ps[:, 0:1], -1.0, float(CAP), ALU.mult, ALU.add), t)
        released[TOTAL] = [left]

        def ranks(src, ready):
            for hf in range(NH):
                part = slice(hf * P, (hf + 1) * P)
                t = vec_op(lambda e, part=part: e.tensor_tensor_scan(scan[:, part], src[:, part], src[:, part], 0.0,
                                                                     ALU.add, ALU.bypass), ready)
            t = vec_op(lambda e: e.tensor_copy(cnt[:, 2:2 + NH], scan[:].rearrange("p (h k) -> p h k", h=NH)[:, :, P - 1]), t)

            def mm(e):
                e.matmul(tot_ps[:, 0:1], earlier_tile[:], cnt[:, 2:3], start=True, stop=True)
                e.matmul(tot_ps[:, 1:2], same_expert[:], cnt[:, 2:3], start=True, stop=False)
                return e.matmul(tot_ps[:, 1:2], earlier_tile[:], cnt[:, 3:4], start=False, stop=True)
            t = pe(mm, t, earlier_ok, *released[TOTAL])
            fill()
            t = vec_op(lambda e: e.tensor_copy(off[:], tot_ps[:, 0:NH]), t)
            released[TOTAL] = [t]
            return t

        t = ranks(eq, t_eq)
        for hf in range(NH):
            part = slice(hf * P, (hf + 1) * P)
            t2 = vec_op(lambda e, part=part, hf=hf: e.tensor_scalar(scan[:, part], scan[:, part], off[:, hf:hf + 1],
                                                                    cnt[:, 1:2], ALU.add, ALU.is_le), t, left)
        t = vec_op(lambda e: e.tensor_tensor(eq[:], eq[:], scan[:], ALU.mult), t2)
        chosen = vec_op(lambda e: e.tensor_tensor(gt[:], gt[:], eq[:], ALU.add), t)
        t = ranks(gt, chosen)
        for hf in range(NH):
            part = slice(hf * P, (hf + 1) * P)
            t2 = vec_op(lambda e, part=part, hf=hf: e.scalar_tensor_tensor(
                out=scan[:, part], in0=scan[:, part], scalar=off[:, hf:hf + 1], in1=gt[:, part], op0=ALU.add,
                op1=ALU.mult), t)
        n = MISC[0]
        t = pe(lambda e: [e.transpose(banks[n][:, hf * P:(hf + 1) * P], scan[:, hf * P:(hf + 1) * P], ident[:])
                          for hf in range(NH)][-1], t2, *released[n])
        fill()
        t = vec_op(lambda e: e.tensor_scalar(slot_i[:], banks[n][:, 0:NT * E], -1.0, None, ALU.add), t, *early_free)
        released[n] = [t]
        t3 = vec_op(lambda e: e.tensor_scalar(eq[:].bitcast(I32), slot_i[:], P - 1, None, ALU.bitwise_and), t)
        t4 = vec_op(lambda e: e.tensor_scalar(gt[:].bitcast(I32), slot_i[:], P.bit_length() - 1, None,
                                              ALU.arith_shift_right), t)
        vec_op(lambda e: e.tensor_copy(slot_c[:].rearrange("p t e -> p (t e)"), eq[:].bitcast(I32)), t3)
        slots_ready = vec_op(lambda e: e.tensor_copy(slot_a[:].rearrange("p t e -> p (t e)"), gt[:].bitcast(I32)), t4)

        pick_zero = put("gpsimd", lambda e: e.memset(pick[:], 0.0), early_free, pool_const)
        pick_free, onehot_free, picked_free = [], [], []
        idx_free, score_free = {n: [] for n in range(NL)}, {n: [] for n in range(NL)}
        marked, listed, gathers, scatters = {}, {}, {}, {}
        xg_free = {k: [(stored[v], 16) for v in (2, 3)] for k in range(2)}

        def mark(ex):
            sa = slot_a[:, :, ex:ex + 1].broadcast_to([P, NT, A])
            t = vec_op(lambda e: e.tensor_tensor(pick[:, :, A:2 * A], sa,
                                                 iota_a[:].unsqueeze(1).broadcast_to([P, NT, A]), ALU.is_equal),
                       slots_ready, iota_ok, pick_zero, *pick_free)
            t2 = vec_op(lambda e: e.tensor_tensor(pick[:, :, 0:A], pick[:, :, A:2 * A],
                                                  tok_id[:].unsqueeze(2).broadcast_to([P, NT, A]), ALU.mult), t)
            t3 = vec_op(lambda e: e.tensor_tensor(pick[:, :, A:2 * A], pick[:, :, A:2 * A],
                                                  probs[:, :, ex:ex + 1].broadcast_to([P, NT, A]), ALU.mult), t2)
            marked[ex] = vec_op(lambda e: e.tensor_tensor(
                onehot[:], slot_c[:, :, ex:ex + 1].broadcast_to([P, NT, P]),
                iota_slot[:].unsqueeze(1).broadcast_to([P, NT, P]), ALU.is_equal), t3, *onehot_free)

        LIST, SLOTS = MISC

        def make_list(ex):
            k = ex % NL

            def mm(e):
                for tile in range(NT):
                    g = tile % G
                    ins = e.matmul(banks[LIST][32 * g:32 * g + 32, 0:P], pick[:, tile, :], onehot[:, tile, :],
                                   start=tile < G, stop=tile >= NT - G)
                return ins
            t = pe(mm, marked[ex], *released[LIST])
            pick_free[:], onehot_free[:] = [t], [t]
            t = vec_op(lambda e: e.tensor_copy(picked[:], banks[LIST][:, 0:P]), t, *picked_free)
            released[LIST] = [t]
            t = pe(lambda e: e.matmul(banks[SLOTS][:, 0:2 * A], picked[:], fold[:, 0:2 * A], start=True, stop=True),
                   t, *released[SLOTS])
            picked_free[:] = [t]
            vec_op(lambda e: e.tensor_copy(idx[:, k, :], banks[SLOTS][:, 0:A]), t, *idx_free[k])
            t = vec_op(lambda e: e.tensor_copy(score[:, k, :], banks[SLOTS][:, A:2 * A]), t, *score_free[k])
            released[SLOTS] = [t]
            listed[ex] = t

        def gather(ex):
            k = ex % 2
            for a in range(A):
                where = bass.IndirectOffsetOnAxis(idx[:, ex % NL, a:a + 1].bitcast(U32), 0)
                t = put("gpsimd", lambda e, a=a, where=where: e.indirect_dma_start(
                    xg[:, k, a, :], None, xn2_dram[:, :], where),
                    [listed[ex], *xg_free[k], *[(s, 16) for s in xn2_stored]], gathered[k], 16)
            gathers[ex] = t

        xgs_free = {0: [], 1: []}
        xgs_ready = {}

        def turn_gathered(ex):
            k = ex % 2
            for c in range(C):
                n = MISC[c]

                def four(e, c=c, n=n):
                    for a in range(A):
                        ins = e.transpose(banks[n][:, a * P:(a + 1) * P], xg[:, k, a, c * P:(c + 1) * P], ident[:])
                    return ins
                t = pe(four, gathers[ex], *released[n])
                hi, lo = xg_s[:, k, 0, c, :], xg_s[:, k, 1, c, :]
                t1 = put("scalar", lambda e, n=n, hi=hi: e.activation(hi, banks[n][:], ACT.Copy),
                         [t, *xgs_free[k]], a_split)
                t2 = vec_op(lambda e, n=n, hi=hi, lo=lo: e.tensor_tensor(lo, banks[n][:], hi.bitcast(F32),
                                                                         ALU.subtract), t1)
                released[n] = [t2]
            xg_free[k] = [t]
            xgs_ready[ex] = t2

        SUM = {0: (4, 5), 1: (0, 1)}
        hid_free = {n: [] for n in range(HC)}
        y_free = {0: [], 1: []}
        hid_ready, sum_done = {}, {}
        out_rows = out.rearrange("b s d -> (b s) d")

        def expert_up(ex, m):
            k, bank, h = ex % 2, UP[m % 2], m % HC

            def mm(e):
                for c in range(C):
                    ins = split_matmul(e, banks[bank][:], lambda i: w1_s[k][:, i, c, m * P:(m + 1) * P],
                                       lambda i: xg_s[:, k, i, c, :], c == 0, c == C - 1)
                return ins
            t = pe(mm, xgs_ready[ex], w_ready["w1", ex], *released[bank])
            cb = col["b1"] + ex * M + m
            t2 = put("scalar", lambda e: e.activation(hid[:, h, :], banks[bank][:], ACT.Gelu_apprx_tanh,
                                                      bias=vec[:, cb:cb + 1]), [t, *hid_free[h]], a_gelu)
            released[bank] = [t2]
            t3 = put("scalar", lambda e: e.activation(hid_s[:, h, 0, :], hid[:, h, :], ACT.Copy), [t2], a_split)
            hid_ready[ex, m] = vec_op(lambda e: e.tensor_tensor(hid_s[:, h, 1, :], hid[:, h, :],
                                                                hid_s[:, h, 0, :].bitcast(F32), ALU.subtract), t3)
            if m == M - 1:
                xgs_free[k] = [t]

        def expert_down(ex, m):
            k, h = ex % 2, m % HC
            sums = SUM[k]

            def mm(e):
                for a in range(A):
                    dst = banks[sums[a // 2]][:, a % 2 * D:(a % 2 + 1) * D]
                    for n, (i, j) in enumerate(((1, 0), (0, 1), (0, 0))):
                        ins = e.matmul(dst, hid_s[:, h, i, a * P:(a + 1) * P], w2_s[k][:, j, m, :],
                                       start=(m == 0 and n == 0 and a % 2 == 0), stop=(m == M - 1 and n == 2),
                                       skip_group_check=True)
                return ins
            t = pe(mm, hid_ready[ex, m], w_ready["w2", ex], *released[sums[0]], *released[sums[1]])
            hid_free[h] = [t]
            sum_done[ex] = t

        def expert_out(ex):
            k = ex % 2
            w_free[k] = [sum_done[ex]]
            rows = []
            for a in range(A):
                bank = SUM[k][a // 2]
                t = vec_op(lambda e, a=a, bank=bank: e.tensor_tensor(
                    y[:, k, a, :], banks[bank][:, a % 2 * D:(a % 2 + 1) * D], b2_rep[:, ex, :], ALU.add),
                    sum_done[ex], b2_loaded, *y_free[k])
                released[bank] = [t]
                rows.append(vec_op(lambda e, a=a: e.tensor_scalar(y[:, k, a, :], y[:, k, a, :], score[:, ex % NL, a:a + 1],
                                                                  None, ALU.mult), t))
            score_free[ex % NL] = [rows[-1]]
            before = [scatters[ex - 1]] if ex else [(s, 16) for s in stored]
            for a in range(A):
                where = bass.IndirectOffsetOnAxis(idx[:, ex % NL, a:a + 1].bitcast(U32), 0)
                t = put("gpsimd", lambda e, a=a, where=where: e.indirect_dma_start(
                    out_rows, where, y[:, k, a, :], None, compute_op=ALU.add), [rows[a], *before], scattered, 16)
            scatters[ex] = t
            y_free[k] = [t]
            idx_free[ex % NL] = [t]

        mark(0)
        fill(2)
        make_list(0)
        mark(1)
        gather(0)
        fill(3)
        make_list(1)
        gather(1)
        b2_loaded = load("b2", b2_rep[:], b2.rearrange("e d -> (e d)").partition_broadcast(P),
                         [(stored[v], 16) for v in (4, 5)])
        fill(len(filler))
        for h in range(HC):
            hid_free[h] = [*u_free[0], *u_free[1]]
        for k in range(2):
            xgs_free[k] = [*tr_free[0], *tr_free[1]]
            y_free[k] = [*u_free[0], *u_free[1]]
        w_free[1] = [*tr_free[1], *u_free[1], (stored[va], 16), (stored[vb], 16)]

        LAG = 2
        turn_gathered(0)
        for m in range(LAG):
            expert_up(0, m)
        split_expert(1)
        for ex in range(E):
            for m in range(M):
                ahead = m + LAG
                if ahead < M:
                    expert_up(ex, ahead)
                elif ex + 1 < E:
                    expert_up(ex + 1, ahead - M)
                expert_down(ex, m)
                if m == 0 and ex + 2 < E:
                    load_expert(ex + 2)
                    mark(ex + 2)
                if m == 2 and ex + 1 < E:
                    turn_gathered(ex + 1)
                if m == 4 and ex + 2 < E:
                    make_list(ex + 2)
                    gather(ex + 2)
            expert_out(ex)
            if ex + 2 < E:
                split_expert(ex + 2)
        put("gpsimd", lambda e: e.nop(), [scatters[E - 1]])

        block = ctx.enter_context(nc.Block())

        @block.sync
        def _(eng):
            plan.run("sync", eng)

        @block.gpsimd
        def _(eng):
            plan.run("gpsimd", eng)

        @block.scalar
        def _(eng):
            plan.run("scalar", eng)

        @block.tensor
        def _(eng):
            plan.run("tensor", eng)

        @block.vector
        def _(eng):
            plan.run("vector", eng)


_INS = ['x', 'ctx_1024', 'mask_BxS2_ik0', 'L0_xattn_Ws', 'L0_xattn_W', 'L0_xattn_w', 'L0_xattn_b', 'L0_xattn_Wcw',
        'L0_xattn_bcw', 'L0_xattn_Wcb', 'L0_xattn_bcb', 'L0_ffn_gate', 'L0_ffn_W1', 'L0_ffn_b1', 'L0_ffn_W2',
        'L0_ffn_b2', 'L0_ffn_Ws1', 'L0_ffn_bs1', 'L0_ffn_Ws2', 'L0_ffn_bs2']


def kernel(**inputs):
    import numpy as _np
    import concourse.bacc as _bacc
    from concourse import mybir as _mybir
    from concourse.bass_utils import run_bass_kernel_spmd as _run

    nc = _bacc.Bacc("TRN2", target_bir_lowering=False, num_devices=1)
    arrays, args = {}, []
    for name in _INS:
        a = _np.ascontiguousarray(inputs[name])
        arrays[f"in_{name}_dram"] = a
        args.append(nc.dram_tensor(f"in_{name}_dram", a.shape, _mybir.dt.from_np(a.dtype), kind="ExternalInput").ap())
    shape = tuple(inputs['x'].shape)
    out = nc.dram_tensor("out_0_dram", shape, _mybir.dt.float32, kind="ExternalOutput").ap()
    xn2 = nc.dram_tensor("xn2_dram", (shape[0] * shape[1], shape[2]), _mybir.dt.float32, kind="Internal").ap()
    xattn_moe_kernel(nc, *args, out, xn2)
    r = _run(nc, [arrays], core_ids=[0])
    return r.results[0]["out_0_dram"]
```

```python
from contextlib import ExitStack

import concourse.bass as bass
from concourse import mybir

F32 = mybir.dt.float32
F32R = mybir.dt.float32r
BF16 = mybir.dt.bfloat16
I32 = mybir.dt.int32
U32 = mybir.dt.uint32
ALU = mybir.AluOpType
ACT = mybir.ActivationFunctionType
AX = mybir.AxisListType

P = 128
BANK = 512
EPS = 1e-5
NEG = 1e30
PAD = -3.0e38
CAP_FACTOR = 1.0
MIN_CAP = 8
RSQRT_MAGIC = 1597463007.0
FIRST_BIT = 29


class Signal:

    def __init__(self, sem):
        self.sem, self.value = sem, 0


class Plan:

    def __init__(self):
        self.queues = {name: [] for name in ("tensor", "vector", "scalar", "gpsimd", "sync")}

    def put(self, engine, emit, after=(), signal=None, by=1):
        self.queues[engine].append((emit, list(after), signal.sem if signal else None, by))
        if signal is None:
            return None
        signal.value += by
        return signal, signal.value

    def run(self, engine, eng):
        reached = {}
        for emit, after, sem, by in self.queues[engine]:
            for signal, value in after:
                if reached.get(id(signal), 0) < value:
                    eng.wait_ge(signal.sem, value)
                    reached[id(signal)] = value
            ins = emit(eng)
            if sem is not None:
                ins.then_inc(sem, by)


BASE, TOP = 16512, 229344

TANH_ADDS, POOL_ADDS = 1, 2
FIRST_TANH_ADDS = (4, 3, 2)

PRE_SLOTS = (2, 4, 7, 7, 9, 9, 10, 11, 12)
TAIL_SLOTS = (1, 1, 3, 3, 5, 6, 6, 6, 8, 10, 11, 13, 13, 14, 15, 16, 16, 18, 18, 20, 20, 21)
LAST_TAIL_SLOTS = (1, 1, 3, 3, 5, 6, 6, 6, 8, 10, 11, 13, 13, 14, 15, 16, 16, 17, 17, 18, 18, 19)
PROJECT_SLOTS = (9, 10)
UP_START = 17
LAST_SLOTS_FREE = 4

LAST_TAIL_FILL = (0, 1, 0, 1, 1, 1, 0, 0, 1, 1, 2, 0, 2, 0, 2, 0, 1, 0, 1, 0, 1, 0)
GELU_AFTER = 7
UP_PIECE = 5
LIST_FILL = (2, 3)


def xattn_moe_kernel(nc, x, ctx_rows, ctx_mask, Ws, W, w, b, Wcw, bcw, Wcb, bcb,
                     gate, W1, b1, W2, b2, Ws1, bs1, Ws2, bs2, out, xn2_dram):
    B, S, D = x.shape
    T = ctx_rows.shape[1]
    E, _, H = W1.shape
    C = D // P
    M = H // P
    TOK = BANK
    J = TOK // P
    UPB = S // TOK
    UNITS = B * UPB
    NTOK = B * S
    NT = NTOK // P
    CAP = max(MIN_CAP, int(CAP_FACTOR * NTOK / E))
    A = CAP // P
    G = 4
    I = -(-T // G)
    R = G * I
    BLOCKS = I
    ZB, XB, NB = 3, 6, 3
    JT = P // E
    NH = NT // JT
    HC = 4
    NL = 3
    assert D % P == 0 and CAP == TOK and I <= 32 and NT % JT == 0 and NH == 2 and UNITS % 2 == 0 and P % E == 0

    plan = Plan()
    put = plan.put

    with ExitStack() as ctx:
        cursor = [BASE]

        def sb(name, shape, dt=F32, at=None):
            n = 1
            for k in shape[1:]:
                n *= k
            where = cursor[0] if at is None else at
            if at is None:
                cursor[0] += -(-n * 4 // 32) * 32
            return nc.alloc_sbuf_tensor_at(name, shape, dt, offset=where)

        def signal(name):
            return Signal(ctx.enter_context(nc.semaphore(name)))

        gate_sb = sb("gate_sb", [P, C, E])
        gate_cols = sb("gate_cols", [P, C, 32])
        bs2_rep = sb("bs2_rep", [P, D])
        mask_rep = sb("mask_rep", [P, B, R])
        cww_rep = sb("cww_rep", [P, B, R])
        cwb_rep = sb("cwb_rep", [P, B, R])
        txt_bias = sb("txt_bias", [P, C, B * T])
        window = sb("window", [P, C, 63])
        ident = sb("ident", [P, P])
        ones = sb("ones", [P, P])
        same_expert = sb("same_expert", [P, P])
        earlier_tile = sb("earlier_tile", [P, P])
        expert_of = sb("expert_of", [P, E])
        fold = sb("fold", [P, 32])
        iota_slot = sb("iota_slot", [P, P])
        iota_a = sb("iota_a", [P, A])
        tok_part = sb("tok_part", [P, 2])
        tok_tile = sb("tok_tile", [P, NT])
        iota_slot_h = sb("iota_slot_h", [P, P], BF16)
        NV = M * E + M + 4 * C
        vec_rows = sb("vec_rows", [NV, P])
        vec = sb("vec", [P, NV])
        bc = sb("bc", [P, 2])
        ln_scratch = [(sb(f"stats{i}", [P, J, 6]), sb(f"mv{i}", [P, J, 2]), sb(f"ve{i}", [P, J]),
                       sb(f"ry{i}", [P, J]), sb(f"ra{i}", [P, J])) for i in range(2)]
        sm = sb("sm", [P, 8, J])
        wb = sb("wb", [P, 2, J])
        lg = sb("lg", [P, J, E])
        lg_t = sb("lg_t", [P, P])
        spare = sb("spare", [P, 2])
        probs = sb("probs", [P, NT, E])
        pt = sb("pt", [P, NH * P])
        eq = sb("eq", [P, NH * P])
        gt = sb("gt", [P, NH * P])
        scan = sb("scan", [P, NH * P])
        cur = sb("cur", [P, 4], I32)
        okbit = sb("okbit", [P, 2], I32)
        cnt = sb("cnt", [P, 8])
        off = sb("off", [P, NH])
        picked = sb("picked", [P, P])
        idx = sb("idx", [P, NL, A], I32)
        score = sb("score", [P, NL, A])

        first = cursor[0]
        z = sb("z", [P, ZB, G * C * TOK])
        feat = sb("feat", [P, 2, C, TOK])
        xn = sb("xn", [P, NB, J, D])
        tr_x = sb("tr_x", [P, C, TOK])
        rho_sb = sb("rho_sb", [P, TOK])
        att = sb("att", [P, J, R])
        att_tmp = sb("att_tmp", [P, J, R])
        w_sb = sb("w_sb", [P, C, D])
        ws_sb = sb("ws_sb", [P, C, D])
        early_end = cursor[0]
        tr_at = cursor[0]
        tr = sb("tr", [P, 2, 2, C, TOK], F32R)
        ws1_at = cursor[0]
        ws1_s = sb("ws1_s", [P, 2, C, H], F32R)
        ws2_sb = sb("ws2_sb", [P, M, D])
        x_at = cursor[0]
        x_ring = sb("x_ring", [P, XB, J, D])
        u_at = cursor[0]
        u = sb("u", [P, 2, M, TOK])
        assert cursor[0] <= TOP, cursor[0]

        cursor[0] = first
        w1_s = [sb("w1_s0", [P, 2, C, H], F32R)]
        w2_s = [sb("w2_s0", [P, 2, M, D], F32R)]
        w1_raw = sb("w1_raw", [P, C, H])
        w2_raw = sb("w2_raw", [P, M, D])
        V = 5
        onehot = sb("onehot", [P, NT, P], BF16)
        pick = sb("pick", [P, NT, 32], BF16)
        in_tile = sb("in_tile", [P, NT, A], BF16)
        vals = sb("vals", [P, NT, E, V], BF16)
        rest = sb("rest", [P, NT, E])
        found = sb("found", [P, V, A])
        slot_i = sb("slot_i", [P, NT * E], I32)
        slot_c = sb("slot_c", [P, NT, E], BF16)
        slot_a = sb("slot_a", [P, NT, E])
        assert cursor[0] <= early_end, (cursor[0], early_end)
        xg_s = sb("xg_s", [P, 2, 2, C, TOK], F32R, at=tr_at)
        w1_s.append(sb("w1_s1", [P, 2, C, H], F32R, at=ws1_at))
        w2_s.append(sb("w2_s1", [P, 2, M, D], F32R, at=ws1_at + 2 * C * H * 4))
        unit_bytes = J * D * 4
        assert ws1_at + 2 * (C * H + M * D) * 4 <= x_at + 2 * unit_bytes
        assert [v % XB for v in (UNITS - 2, UNITS - 1)] == [0, 1]
        xg = sb("xg", [P, 2, A, D], at=x_at + 2 * unit_bytes)
        b2_rep = sb("b2_rep", [P, E, D], at=x_at + 4 * unit_bytes)
        cursor[0] = u_at
        hid = sb("hid", [P, HC, TOK])
        hid_s = sb("hid_s", [P, HC, 2, TOK], F32R)
        y = sb("y", [P, 2, A, D])
        assert cursor[0] <= TOP
        ctx_sb = z[0:T, 2, 0:B * D].rearrange("p (b d) -> p b d", b=B)
        txt_t = z[:, 2, B * D:B * D + C * B * T].rearrange("p (c n) -> p c n", c=C)
        wide = z[:, 2, 2048:2048 + 2 * C * P].rearrange("p (v c m) -> p v c m", v=2, c=C)
        row = z[:, 2, 2560:2560 + 3 * B * R].rearrange("p (v b r) -> p v b r", v=3, b=B)
        mask_i = z[:, 2, 2560 + 3 * B * R:2560 + 3 * B * R + B * T].bitcast(I32)
        assert 2560 + 3 * B * R + B * T <= G * C * TOK
        ws1_raw = u[:, 1, 0:C * H // TOK, :].rearrange("p m s -> p (m s)").rearrange("p (c h) -> p c h", c=C)

        banks = [ctx.enter_context(nc.psum_tensor(f"bank{i}", [P, BANK], F32)) for i in range(8)]
        RHO, UP, DOWN, MISC = (0, 1), (2, 3), (4, 5), (6, 7)
        released = {i: [] for i in range(8)}

        loaded = {}

        def load(name, dst, src, after=()):
            s = signal(f"ld_{name}")
            loaded[name] = put("sync", lambda e: e.dma_start(dst, src), after, s, 16)
            return loaded[name]

        pool_const = signal("pool_const")
        pool_add = signal("pool_add")
        pool_small = signal("pool_small")
        pool_split = signal("pool_split")
        v_chain = signal("v_chain")
        v_add = signal("v_add")
        a_tanh = signal("a_tanh")
        a_small = signal("a_small")
        a_gelu = signal("a_gelu")
        a_split = signal("a_split")
        t_rho = signal("t_rho")
        t_work = signal("t_work")
        stored = [signal(f"stored{i}") for i in range(UNITS)]
        xn2_stored = [signal(f"xn2_stored{i}") for i in range(UNITS)]
        gathered = [signal(f"gathered{i}") for i in range(2)]
        scattered = signal("scattered")

        def vec_op(emit, *after):
            return put("vector", emit, after, v_chain)

        def pe(emit, *after):
            return put("tensor", emit, after, t_work)

        SPLIT_TERMS = ((1, 0), (0, 1), (0, 0))

        def split_matmul(e, dst, lhs, rhs, start, stop):
            for n, (a, c) in enumerate(SPLIT_TERMS):
                ins = e.matmul(dst, lhs(a), rhs(c), start=start and n == 0, stop=stop and n == len(SPLIT_TERMS) - 1)
            return ins

        def load_x(v, after=()):
            xr = x[v // UPB, (v % UPB) * TOK:(v % UPB + 1) * TOK, :].rearrange("(j p) d -> p j d", p=P)
            return load(f"x{v}", x_ring[:, v % XB], xr, after)

        load_x(0)
        load("w", w_sb[:], W.rearrange("(c p) d -> p c d", p=P))
        load("ctx", ctx_sb, ctx_rows.rearrange("b t d -> t b d"))
        load("ws", ws_sb[:], Ws.rearrange("(c p) d -> p c d", p=P))
        vec_sources = [("b1", b1.rearrange("e (m p) -> (e m) p", p=P)),
                       ("bs1", bs1.rearrange("(m p) -> m p", p=P)),
                       ("b", b.rearrange("a (c p) -> (a c) p", p=P)),
                       ("Wcw", Wcw.rearrange("a (c p) -> (a c) p", p=P)),
                       ("Wcb", Wcb.rearrange("a (c p) -> (a c) p", p=P)),
                       ("w_col", w.rearrange("(c p) a -> (c a) p", p=P))]
        at, col = 0, {}
        for name, src in vec_sources:
            n = src.shape[0]
            load("v_" + name, vec_rows[at:at + n, :], src)
            col[name] = at
            at += n
        assert at == NV
        load("mask", mask_i, ctx_mask.rearrange("b t -> (b t)").partition_broadcast(P))
        load("bcw", bc[:, 0:1], bcw.partition_broadcast(P))
        load("bcb", bc[:, 1:2], bcb.partition_broadcast(P))
        load("gate", gate_sb[:], gate.rearrange("(c p) e -> p c e", p=P))
        load("bs2", bs2_rep[:], bs2.partition_broadcast(P))
        load_x(1)
        load("ws1", ws1_raw, Ws1.rearrange("(c p) h -> p c h", p=P))
        load("ws2", ws2_sb[:], Ws2.rearrange("(m p) d -> p m d", p=P))
        for v in range(2, XB):
            load_x(v)

        def const(emit, *after):
            return put("gpsimd", emit, after, pool_const)

        c0 = const(lambda e: e.memset(ident[:], 0.0))
        ident_ok = const(lambda e: e.affine_select(out=ident[:], in_=ident[:], compare_op=ALU.not_equal, fill=1.0,
                                                   base=0, pattern=[[-1, P]], channel_multiplier=1), c0)
        ones_ok = const(lambda e: e.memset(ones[:], 1.0))
        spare_ok = const(lambda e: e.memset(spare[:], 0.0))
        row_ok = const(lambda e: e.memset(row, 0.0))
        win0 = const(lambda e: e.memset(window[:], 0.0))
        cols0 = const(lambda e: e.memset(gate_cols[:], 0.0))
        const(lambda e: e.iota(iota_slot[:], [[1, P]], base=0, channel_multiplier=0,
                               allow_small_or_imprecise_dtypes=True))
        const(lambda e: e.iota(iota_a[:], [[1, A]], base=0, channel_multiplier=0,
                               allow_small_or_imprecise_dtypes=True))
        const(lambda e: e.iota(tok_part[:], [[0, 2]], base=0, channel_multiplier=1,
                               allow_small_or_imprecise_dtypes=True))
        iota_ok = const(lambda e: e.iota(tok_tile[:], [[1, NT]], base=0, channel_multiplier=0,
                                         allow_small_or_imprecise_dtypes=True))

        def moments(src, scratch, *after):
            for j in range(J):
                t = vec_op(lambda e, j=j: e.bn_stats(scratch[0][:, j, :], src[:, j, :]), *after)
            return t

        def rsqrt_guess(scratch, *after):
            stats, mv, ve, ry, _ = scratch
            for j in range(J):
                t = vec_op(lambda e, j=j: e.bn_aggr(mv[:, j, :], stats[:, j, :]), *after)
            t = vec_op(lambda e: e.tensor_scalar(ve[:], mv[:, :, 1], EPS, None, ALU.add), t)
            t = vec_op(lambda e: e.tensor_scalar(ry[:].bitcast(I32), ve[:].bitcast(I32), 1, None,
                                                 ALU.logical_shift_right), t)
            return vec_op(lambda e: e.tensor_scalar(ry[:].bitcast(I32), ry[:].bitcast(I32), -1.0, RSQRT_MAGIC,
                                                    ALU.mult, ALU.add), t)

        def newton(scratch, on_pool, *after):
            _, _, ve, ry, ra = scratch
            t = after[-1]
            if on_pool:
                def op(emit, *after):
                    return put("gpsimd", emit, after, pool_small)
            else:
                op = vec_op
            for _ in range(3):
                t = op(lambda e: e.tensor_tensor(ra[:], ry[:], ry[:], ALU.mult), t)
                t = op(lambda e: e.tensor_tensor(ra[:], ra[:], ve[:], ALU.mult), t)
                t = op(lambda e: e.tensor_scalar(ra[:], ra[:], -0.5, 1.5, ALU.mult, ALU.add), t)
                t = op(lambda e: e.tensor_tensor(ry[:], ra[:], ry[:], ALU.mult), t)
            return t

        def normalise(src, dst, scratch, *after):
            _, mv, _, ry, _ = scratch
            for j in range(J):
                t = vec_op(lambda e, j=j: e.tensor_scalar(dst[:, j, :], src[:, j, :], mv[:, j, 0:1], ry[:, j:j + 1],
                                                          ALU.subtract, ALU.mult), *after)
            return t

        def transposes(bank, src, c, *after):
            def four(e):
                for j in range(J):
                    ins = e.transpose(banks[bank][:, j * P:(j + 1) * P], src[:, j, c * P:(c + 1) * P], ident[:])
                return ins
            return pe(four, ident_ok, *after, *released[bank])

        feat_ready, tr_ready, x2_ready, probs_ready, rho_last, up_done = {}, {}, {}, {}, {}, {}
        feat_free = {0: [], 1: []}
        xn_free = {n: [] for n in range(NB)}
        tr_free = {0: [], 1: []}
        tr_x_free, rho_sb_free, lg_t_free = [], [], []
        u_free = {0: [], 1: []}

        def pre_steps(v):
            src, dst = x_ring[:, v % XB], xn[:, v % NB]
            hold = {}

            def stats():
                hold["t"] = moments(src, ln_scratch[0], loaded[f"x{v}"])

            def rsqrt():
                t = rsqrt_guess(ln_scratch[0], hold["t"])
                hold["t"] = newton(ln_scratch[0], True, t)

            def apply():
                hold["t"] = normalise(src, dst, ln_scratch[0], hold["t"], *xn_free[v % NB])

            def turn():
                hold["t"] = [transposes(MISC[c], dst, c, hold["t"]) for c in range(C)]

            def turned():
                for c in range(C):
                    t = vec_op(lambda e, c=c: e.tensor_copy(tr_x[:, c, :], banks[MISC[c]][:]), hold["t"][c],
                               *tr_x_free)
                    released[MISC[c]] = [t]
                hold["tr"] = t

            def project(co):
                def mm(e):
                    for c in range(C):
                        ins = e.matmul(banks[MISC[co]][:], w_sb[:, c, co * P:(co + 1) * P], tr_x[:, c, :],
                                       start=c == 0, stop=c == C - 1)
                    return ins
                hold[co] = pe(mm, hold["tr"], loaded["w"], *released[MISC[co]])
                tr_x_free[:] = [hold[co]]

            def projected(co):
                t = vec_op(lambda e: e.tensor_copy(feat[:, v % 2, co, :], banks[MISC[co]][:]), hold[co],
                           *feat_free[v % 2])
                released[MISC[co]] = [t]
                feat_ready[v] = t

            return ([stats, rsqrt, apply, turn, turned] + [lambda co=co: project(co) for co in range(C)]
                    + [lambda co=co: projected(co) for co in range(C)])

        def tail_steps(v):
            xs, ns = x_ring[:, v % XB], xn[:, v % NB]
            batch, rho_bank = v // UPB, RHO[v % 2]
            hold = {}

            def evacuate():
                hold["t"] = vec_op(lambda e: e.tensor_copy(rho_sb[:], banks[rho_bank][:]), rho_last[v], *rho_sb_free)
                released[rho_bank] = [hold["t"]]

            def to_tokens():
                n = MISC[0]

                def four(e):
                    for j in range(J):
                        ins = e.transpose(banks[n][:, j * P:(j + 1) * P], rho_sb[:, j * P:(j + 1) * P], ident[:])
                    return ins
                hold["t"] = pe(four, hold["t"], ident_ok, *released[n])
                rho_sb_free[:] = [hold["t"]]

            def shift():
                n = MISC[0]
                rt = banks[n][:].rearrange("p (j g i) -> p j g i", j=J, g=G)
                t = vec_op(lambda e: e.tensor_tensor(
                    att[:].rearrange("p j (g i) -> p j g i", g=G), rt[:, :, :, 0:I],
                    mask_rep[:, batch, :].rearrange("p (g i) -> p g i", g=G).unsqueeze(1).broadcast_to([P, J, G, I]),
                    ALU.add), hold["t"])
                released[n] = [t]
                t = vec_op(lambda e: e.tensor_reduce(sm[:, 0, :], att[:], AX.X, ALU.max), t)
                hold["t"] = vec_op(lambda e: e.tensor_tensor(
                    att[:], att[:], sm[:, 0, :].unsqueeze(2).broadcast_to([P, J, R]), ALU.subtract), t)

            def exp():
                hold["t"] = put("scalar", lambda e: e.activation(att[:], att[:], ACT.Exp), [hold["t"]], a_small)

            def weigh(n, rep):
                t = hold["t"]
                if n == 0:
                    t = vec_op(lambda e: e.tensor_reduce(sm[:, 1, :], att[:], AX.X, ALU.add), t)
                    vec_op(lambda e: e.reciprocal(sm[:, 2, :], sm[:, 1, :]), t)
                t = vec_op(lambda e: e.tensor_tensor(
                    att_tmp[:], att[:], rep[:, batch, :].unsqueeze(1).broadcast_to([P, J, R]), ALU.mult), t)
                hold["t"] = vec_op(lambda e: e.tensor_reduce(wb[:, n, :], att_tmp[:], AX.X, ALU.add), t)

            def gate_inputs():
                t = vec_op(lambda e: e.tensor_tensor(wb[:], wb[:], sm[:, 2, :].unsqueeze(1).broadcast_to([P, 2, J]),
                                                     ALU.mult), hold["t"])
                hold["t"] = vec_op(lambda e: e.tensor_tensor(wb[:], wb[:], bc[:].unsqueeze(2).broadcast_to([P, 2, J]),
                                                             ALU.add), t, loaded["bcw"], loaded["bcb"])

            def gates():
                hold["t"] = put("scalar", lambda e: e.activation(wb[:], wb[:], ACT.Tanh), [hold["t"]], a_small)

            def residual():
                for j in range(J):
                    t = vec_op(lambda e, j=j: e.scalar_tensor_tensor(
                        out=xs[:, j, :], in0=ns[:, j, :], scalar=wb[:, 0, j:j + 1], in1=xs[:, j, :], op0=ALU.mult,
                        op1=ALU.add), hold["t"])
                hold["t"] = t

            def stats():
                hold["t"] = moments(xs, ln_scratch[1], hold["t"])

            def rsqrt():
                t = rsqrt_guess(ln_scratch[1], hold["t"])
                hold["t"] = newton(ln_scratch[1], v + 1 < UNITS, t)

            def whole():
                for j in range(J):
                    x2_ready[v] = vec_op(lambda e, j=j: e.scalar_tensor_tensor(
                        out=xs[:, j, :], in0=xs[:, j, :], scalar=wb[:, 1, j:j + 1], in1=bs2_rep[:], op0=ALU.add,
                        op1=ALU.add), hold["normal"], loaded["bs2"])

            def apply():
                t = normalise(xs, ns, ln_scratch[1], hold["t"])
                hold["t"] = hold["normal"] = t
                hold["store"] = put("sync", lambda e: e.dma_start(
                    xn2_dram[v * TOK:(v + 1) * TOK, :].rearrange("(j p) d -> p j d", p=P), ns),
                    [t], xn2_stored[v], 16)

            def turn():
                hold["t"] = [transposes(MISC[c], ns, c, hold["t"]) for c in range(C)]
                xn_free[v % NB] = [hold["t"][-1], hold["store"]]

            def turned(c):
                src = banks[MISC[c]]
                t = vec_op(lambda e: e.tensor_copy(tr[:, v % 2, 0, c, :], src[:]), hold["t"][c], *tr_free[v % 2])
                t = vec_op(lambda e: e.tensor_tensor(
                    tr[:, v % 2, 1, c, :], src[:], tr[:, v % 2, 0, c, :].bitcast(F32), ALU.subtract), t)
                released[MISC[c]] = [t]
                tr_ready[v] = t

            def logits():
                n = MISC[0]

                def mm(e):
                    for c in range(C):
                        for i in (1, 0):
                            for j in range(J):
                                ins = e.matmul(banks[n][32 * j:32 * j + 32, 0:P], gate_cols[:, c, :],
                                               tr[:, v % 2, i, c, j * P:(j + 1) * P].bitcast(F32),
                                               start=c == 0 and i == 1, stop=c == C - 1 and i == 0)
                    return ins
                hold["t"] = pe(mm, tr_ready[v], gate_ok[0], *released[n])
                tr_free[v % 2] = [hold["t"]]

            def keep_logits():
                n = MISC[0]
                hold["t"] = vec_op(lambda e: e.tensor_copy(lg_t[:], banks[n][:, 0:P]), hold["t"], *lg_t_free)
                released[n] = [hold["t"]]

            def turn_logits():
                n = MISC[1]
                hold["t"] = pe(lambda e: e.transpose(banks[n][:, 0:P], lg_t[:], ident[:]), hold["t"], *released[n])
                lg_t_free[:] = [hold["t"]]

            def shift_logits():
                n = MISC[1]
                lp = banks[n][:, 0:P].rearrange("p (j e) -> p j e", j=J)[:, :, 0:E]
                t = vec_op(lambda e: e.tensor_reduce(sm[:, 3, :], lp, AX.X, ALU.max), hold["t"])
                hold["t"] = vec_op(lambda e: e.tensor_tensor(
                    lg[:], lp, sm[:, 3, :].unsqueeze(2).broadcast_to([P, J, E]), ALU.subtract), t)
                released[n] = [hold["t"]]

            def exp_logits():
                hold["t"] = put("scalar", lambda e: e.activation(lg[:], lg[:], ACT.Exp), [hold["t"]], a_small)

            def router():
                t = vec_op(lambda e: e.tensor_reduce(sm[:, 4, :], lg[:], AX.X, ALU.add), hold["t"])
                t = vec_op(lambda e: e.reciprocal(sm[:, 5, :], sm[:, 4, :]), t)
                probs_ready[v] = vec_op(lambda e: e.tensor_tensor(
                    probs[:, v * J:(v + 1) * J, :], lg[:], sm[:, 5, :].unsqueeze(2).broadcast_to([P, J, E]),
                    ALU.mult), t)

            return [evacuate, to_tokens, shift, exp, lambda: weigh(0, cww_rep), lambda: weigh(1, cwb_rep),
                    gate_inputs, gates, residual, stats, rsqrt, apply, turn, whole,
                    *[lambda c=c: turned(c) for c in range(C)], logits, keep_logits, turn_logits, shift_logits, exp_logits, router]

        def up_product(v, m, bank, after):
            def mm(e):
                for c in range(C):
                    ins = split_matmul(e, banks[bank][:], lambda i: ws1_s[:, i, c, m * P:(m + 1) * P],
                                       lambda i: tr[:, v % 2, i, c, :], c == 0, c == C - 1)
                return ins
            return pe(mm, *after)

        def up_steps(v):
            hold = {}

            def product(m):
                bank = UP[m % 2]
                hold[m] = up_product(v, m, bank, [tr_ready[v], ws1_ok[0], *released[bank]])
                tr_free[v % 2] = [hold[m]]

            def biased(m):
                bank = UP[m % 2]
                up_done[v] = vec_op(lambda e: e.tensor_scalar(
                    u[:, v % 2, m, :], banks[bank][:], vec[:, col["bs1"] + m:col["bs1"] + m + 1], None, ALU.add),
                    hold[m], vec_ready[0], *u_free[v % 2])
                released[bank] = [up_done[v]]

            return [lambda m=m: product(m) for m in range(M)], [lambda m=m: biased(m) for m in range(M)]

        gelu_done = {}

        def gelu(v):
            part = u[:, v % 2]
            gelu_done[v] = put("scalar", lambda e: e.activation(part, part, ACT.Gelu_apprx_tanh), [up_done[v]], a_gelu)

        def down_product(v, j, bank, chunks, after):
            def mm(e):
                for m in chunks:
                    ins = e.matmul(banks[bank][:, 0:D], u[:, v % 2, m, j * P:(j + 1) * P], ws2_sb[:, m, :],
                                   start=m == 0, stop=m == M - 1)
                return ins
            return pe(mm, *after)

        def down_end(v, j, bank, t):
            xs = x_ring[:, v % XB]
            done = vec_op(lambda e: e.tensor_tensor(xs[:, j, :], banks[bank][:, 0:D], xs[:, j, :], ALU.add), t,
                          x2_ready[v])
            released[bank] = [done]
            if j == J - 1:
                u_free[v % 2] = [t]
                rows = out[v // UPB, (v % UPB) * TOK:(v % UPB + 1) * TOK, :]
                s = put("sync", lambda e: e.dma_start(rows.rearrange("(j p) d -> p j d", p=P), xs), [done],
                        stored[v], 16)
                if v + XB < UNITS:
                    load_x(v + XB, [s])

        def down_steps(v, cuts):
            hold = {}

            def product(j, n):
                bank = DOWN[j % 2]
                hold[j] = down_product(v, j, bank, range(cuts[n], cuts[n + 1]),
                                       [gelu_done[v], loaded["ws2"], *(released[bank] if n == 0 else [])])

            return ([lambda j=j, n=n: product(j, n) for j in range(J) for n in range(len(cuts) - 1)],
                    [lambda j=j: down_end(v, j, DOWN[j % 2], hold[j]) for j in range(J)])

        first_steps = pre_steps(0)
        for step in first_steps[:2]:
            step()

        t = pe(lambda e: e.transpose(banks[2][:, 0:NV], vec_rows[:], ident[0:NV, 0:NV]), ident_ok,
               *[loaded["v_" + name] for name, _ in vec_sources])
        vec_ready = [vec_op(lambda e: e.tensor_copy(vec[:], banks[2][:, 0:NV]), t)]
        released[2] = vec_ready[:]
        window_ready = [vec_op(lambda e: e.tensor_copy(window[:, :, 31], vec[:, col["w_col"]:col["w_col"] + C]),
                               vec_ready[0], win0)]

        def ctx_transposes(e, c):
            for bb in range(B):
                ins = e.transpose(banks[4 + c][:, bb * T:(bb + 1) * T], ctx_sb[:, bb, c * P:(c + 1) * P],
                                  ident[0:T, 0:T])
            return ins
        for c in range(C):
            t = pe(lambda e, c=c: ctx_transposes(e, c), loaded["ctx"], ident_ok)
            t = vec_op(lambda e, c=c: e.tensor_copy(txt_t[:, c, :], banks[4 + c][:, 0:B * T]), t)
            released[4 + c] = [t]
        txt_t_ready = t
        ctx_products = []
        for co in range(C):
            def mm(e, co=co):
                for c in range(C):
                    ins = e.matmul(banks[2 + co][:, 0:B * T], ws_sb[:, c, co * P:(co + 1) * P], txt_t[:, c, :],
                                   start=c == 0, stop=c == C - 1)
                return ins
            ctx_products.append(pe(mm, txt_t_ready, loaded["ws"], *released[2 + co]))
        for step in first_steps[2:5]:
            step()
        for co, t in enumerate(ctx_products):
            t = vec_op(lambda e, co=co: e.tensor_scalar(txt_bias[:, co, :], banks[2 + co][:, 0:B * T],
                                                        vec[:, col["b"] + co:col["b"] + co + 1], None, ALU.add), t,
                       vec_ready[0])
            released[2 + co] = [t]
        txt_ready = [t]
        for step in first_steps[5:]:
            step()

        z_free = {n: [] for n in range(ZB)}
        added, tanhed = {}, {}
        LAST = UNITS * BLOCKS

        def block_of(n):
            v, k = n // BLOCKS, n % BLOCKS
            return v, k, [t for t in range(G * k, G * k + G) if t < T]

        def tanh_adds(n):
            return FIRST_TANH_ADDS[n] if n < len(FIRST_TANH_ADDS) else TANH_ADDS

        def add_block(n):
            v, k, rows = block_of(n)
            zb = z[:, n % ZB, :].rearrange("p (r c s) -> p r c s", r=G, c=C)
            done = {}

            for r, t in enumerate(rows):
                for c in range(C):
                    if r * C + c >= G * C - tanh_adds(n):
                        continue
                    pool = r * C + c >= G * C - tanh_adds(n) - POOL_ADDS
                    emit = lambda e, r=r, t=t, c=c, pool=pool: e.tensor_scalar(
                        zb[:, r, c, :], feat[:, v % 2, c, :], txt_bias[:, c, v // UPB * T + t:v // UPB * T + t + 1],
                        1.0 if pool else None, ALU.add, *([ALU.mult] if pool else []))
                    after = [feat_ready[v], txt_ready[0], *z_free[n % ZB]]
                    if pool:
                        done["pool"] = put("gpsimd", emit, after, pool_add)
                    else:
                        done["vector"] = put("vector", emit, after, v_add)
            added[n] = list(done.values())

        def tanh_block(n):
            v, _, rows = block_of(n)
            whole = min(len(rows) * C, G * C - tanh_adds(n))
            for i in range(whole, len(rows) * C):
                r, c = i // C, i % C
                t = rows[r]
                put("scalar", lambda e, i=i, t=t, c=c: e.activation(
                    z[:, n % ZB, i * TOK:(i + 1) * TOK], feat[:, v % 2, c, :], ACT.Tanh,
                    bias=txt_bias[:, c, v // UPB * T + t:v // UPB * T + t + 1]),
                    [feat_ready[v], txt_ready[0], *z_free[n % ZB]], a_tanh)
            part = z[:, n % ZB, 0:whole * TOK]
            tanhed[n] = put("scalar", lambda e: e.activation(part, part, ACT.Tanh), added[n], a_tanh)

        def rho_block(n):
            v, k, rows = block_of(n)
            zb = z[:, n % ZB, :].rearrange("p (r c s) -> p r c s", r=G, c=C)
            bank = RHO[v % 2]

            def mm(e):
                for c in range(C):
                    for r, t in enumerate(rows):
                        ins = e.matmul(banks[bank][32 * r:32 * r + 32, :], window[:, c, 31 - k:63 - k],
                                       zb[:, r, c, :], start=(c == 0 and k == 0), stop=(c == C - 1 and t + G >= T))
                return ins

            tok = put("tensor", mm, [tanhed[n], window_ready[0], *(released[bank] if k == 0 else [])], t_rho)
            z_free[n % ZB] = [tok]
            rho_last[v] = tok

        add_block(0)
        tanh_block(0)
        add_block(1)

        for v, name in enumerate(("Wcw", "Wcb")):
            for c in range(C):
                t = vec_op(lambda e, v=v, c=c, name=name: e.tensor_scalar(
                    wide[:, v, c, :], ones[:], vec[:, col[name] + c:col[name] + c + 1], None, ALU.mult),
                    vec_ready[0], ones_ok)
        wide_ready = t
        t = vec_op(lambda e: e.tensor_scalar(row[:, 0, :, 0:T], mask_i.rearrange("p (b t) -> p b t", b=B), 1.0, NEG,
                                             ALU.subtract, ALU.mult), loaded["mask"], row_ok)
        if R > T:
            vec_op(lambda e: e.memset(row[:, 0, :, T:R], PAD), row_ok)
        for v in range(2):
            def mm(e, v=v):
                for c in range(C):
                    ins = e.matmul(banks[DOWN[v]][:, 0:B * T], wide[:, v, c, :], txt_t[:, c, :],
                                   start=c == 0, stop=c == C - 1)
                return ins
            t = pe(mm, wide_ready, txt_t_ready, *released[DOWN[v]])
            t = vec_op(lambda e, v=v: e.tensor_copy(row[:, 1 + v, :, 0:T],
                                                    banks[DOWN[v]][:, 0:B * T].rearrange("p (b t) -> p b t", b=B)),
                       t, row_ok)
            released[DOWN[v]] = [t]
        for v, rep in enumerate((mask_rep, cww_rep, cwb_rep)):
            t2 = vec_op(lambda e, v=v, rep=rep: e.tensor_copy(
                rep[:].rearrange("p b (g i) -> p b g i", g=G), row[:, v, :, :].rearrange("p b (i g) -> p b g i", g=G)),
                t)
        z_free[2] = [t2]

        gate_ok = [vec_op(lambda e: e.tensor_copy(gate_cols[:, :, 0:E], gate_sb[:]), loaded["gate"], cols0)]
        vec_op(lambda e: e.tensor_copy(iota_slot_h[:], iota_slot[:]), iota_ok)
        t = vec_op(lambda e: e.tensor_reduce(expert_of[:], ident[:].rearrange("p (t e) -> p e t", e=E), AX.X, ALU.add),
                   ident_ok)
        vec_op(lambda e: e.tensor_reduce(fold[:], ident[:].rearrange("p (g r) -> p r g", r=32), AX.X, ALU.add),
               ident_ok)
        router_consts = vec_op(lambda e: e.tensor_copy(same_expert[:].rearrange("p (t e) -> p t e", e=E),
                                                       expert_of[:].unsqueeze(1).broadcast_to([P, JT, E])), t)
        earlier_ok = const(lambda e: e.affine_select(out=earlier_tile[:], in_=same_expert[:], compare_op=ALU.is_gt,
                                                     fill=0.0, base=0, pattern=[[1, P]], channel_multiplier=-1),
                           router_consts)

        ws1_ok = []

        def split_ws1(c):
            t = vec_op(lambda e: e.tensor_copy(ws1_s[:, 0, c, :], ws1_raw[:, c, :]), loaded["ws1"])
            ws1_ok[:] = [vec_op(lambda e: e.tensor_tensor(ws1_s[:, 1, c, :], ws1_raw[:, c, :],
                                                          ws1_s[:, 0, c, :].bitcast(F32), ALU.subtract), t)]
            u_free[1] = ws1_ok[:]

        slots = {}

        def at_slots(unit, places, steps):
            for place, step in zip(places, steps, strict=True):
                slots.setdefault(unit * BLOCKS + place, []).append(step)

        at_slots(0, [10, 11], [lambda c=c: split_ws1(c) for c in range(C)])
        for v in range(UNITS):
            if v > 0:
                at_slots(v - 1, PRE_SLOTS, pre_steps(v))
            if v + 1 < UNITS:
                at_slots(v + 1, TAIL_SLOTS if v + 2 < UNITS else LAST_TAIL_SLOTS, tail_steps(v))
            if v % 2 == 1 and v + 1 < UNITS:
                for unit, start in ((v - 1, 0), (v, UP_START)):
                    products, biased = up_steps(unit)
                    at_slots(v + 1, range(start + 2, start + 2 + M), biased)
                    at_slots(v + 1, range(start, start + M), products)
                gelu_at = UP_START + M + 1
                at_slots(v + 1, [gelu_at] * 2, [lambda unit=unit: gelu(unit) for unit in (v - 1, v)])
                another = v + 3 < UNITS
                clear = [p for p in range(gelu_at + 1, 5 * BLOCKS) if p % BLOCKS not in PROJECT_SLOTS[:1 + (p > gelu_at + 9)]
                         and not (another and 2 * BLOCKS <= p < 2 * BLOCKS + M)
                         and not (not another and 2 * BLOCKS - LAST_SLOTS_FREE <= p < 2 * BLOCKS)]
                for unit in (v - 1, v):
                    cuts = (0, 3, 6, M) if another and unit == v - 1 else (0, M // 2, M)
                    n = len(cuts) - 1
                    products, ends = down_steps(unit, cuts)
                    busy, clear = clear[:n * J], clear[n * J:]
                    at_slots(v + 1, [p + 2 for p in busy[n - 1::n]], ends)
                    at_slots(v + 1, busy, products)

        for n in range(LAST):
            v, k, _ = block_of(n)
            if n + 2 < LAST:
                add_block(n + 2)
            if n + 1 < LAST:
                tanh_block(n + 1)
            rho_block(n)
            for step in slots.pop(n, []):
                step()
            if n + 2 < LAST and (n + 2) % BLOCKS == BLOCKS - 1:
                feat_free[(n + 2) // BLOCKS % 2] = added[n + 2] + added[n + 1]
            if n + 1 < LAST and (n + 1) % BLOCKS == BLOCKS - 1:
                feat_free[(n + 1) // BLOCKS % 2] += [tanhed[n + 1]]
        va, vb = UNITS - 2, UNITS - 1
        filler = [lambda steps=slots[n]: [step() for step in steps] for n in sorted(slots)]
        ends = []

        def fill(n=1):
            for _ in range(n):
                due = ends[:]
                ends.clear()
                if filler:
                    filler.pop(0)()
                for end in due:
                    end()

        def up_identity(m):
            bank = UP[m % 2]
            t = up_product(va, m, bank, [tr_ready[va], ws1_ok[0], *released[bank]])
            tr_free[va % 2] = [t]
            up_done[va] = put("scalar", lambda e: e.activation(
                u[:, va % 2, m, :], banks[bank][:], ACT.Identity, bias=vec[:, col["bs1"] + m:col["bs1"] + m + 1]),
                [t, vec_ready[0], *u_free[va % 2]], a_gelu)
            released[bank] = [up_done[va]]

        PASSES = len(SPLIT_TERMS) * C

        def up_gelu(passes):
            for m in sorted({n // PASSES for n in passes}):
                mine = [n % PASSES for n in passes if n // PASSES == m]
                bank = UP[m % 2]

                def mm(e, m=m, mine=mine, bank=bank):
                    for n in mine:
                        c, (i, j) = n // len(SPLIT_TERMS), SPLIT_TERMS[n % len(SPLIT_TERMS)]
                        ins = e.matmul(banks[bank][:], ws1_s[:, i, c, m * P:(m + 1) * P], tr[:, vb % 2, j, c, :],
                                       start=n == 0, stop=n == PASSES - 1)
                    return ins
                t = pe(mm, tr_ready[vb], *(released[bank] if mine[0] == 0 else []))
                tr_free[vb % 2] = [t]
                if mine[-1] == PASSES - 1:
                    gelu_done[vb] = put("scalar", lambda e, m=m, bank=bank: e.activation(
                        u[:, vb % 2, m, :], banks[bank][:], ACT.Gelu_apprx_tanh,
                        bias=vec[:, col["bs1"] + m:col["bs1"] + m + 1]), [t, *u_free[vb % 2]], a_gelu)
                    released[bank] = [gelu_done[vb]]

        def down_piece(v, j, n):
            bank = DOWN[j % 2]
            t = down_product(v, j, bank, range(2 * n, 2 * n + 2),
                             [gelu_done[v], loaded["ws2"], *(released[bank] if n == 0 else [])])
            if 2 * n + 2 == M:
                ends.append(lambda: down_end(v, j, bank, t))

        def down_pieces(v):
            return [lambda j=j, n=n: down_piece(v, j, n) for j in range(J) for n in range(M // 2)]

        leftover = filler[:]
        filler[:] = [lambda m=m: up_identity(m) for m in range(M)]
        for i, step in enumerate(tail_steps(vb)):
            step()
            fill(LAST_TAIL_FILL[i])
            if i == GELU_AFTER:
                fill(M - sum(LAST_TAIL_FILL[:i + 1]))
                gelu(va)
                put("scalar", lambda e: e.activation(spare[:, 1:2], spare[:, 0:1], ACT.Exp), [spare_ok], a_small)
                filler += leftover + down_pieces(va)
        filler += [lambda n=n: up_gelu(range(n, min(n + UP_PIECE, M * PASSES))) for n in range(0, M * PASSES, UP_PIECE)]
        filler += down_pieces(vb)
        early_free = [probs_ready[vb], tanhed[LAST - 1], rho_last[vb], tr_ready[vb], (xn2_stored[vb], 16)]

        w_free = {0: list(early_free), 1: []}
        w_ready = {}
        raw_free = {"w1": list(early_free), "w2": list(early_free)}

        def load_expert(ex):
            load(f"w1_{ex}", w1_raw[:], W1[ex].rearrange("(c p) h -> p c h", p=P), raw_free["w1"])
            load(f"w2_{ex}", w2_raw[:], W2[ex].rearrange("(m p) d -> p m d", p=P), raw_free["w2"])

        def split_expert(ex):
            k = ex % 2
            for name, raw, parts in (("w1", w1_raw, w1_s[k]), ("w2", w2_raw, w2_s[k])):
                t = put("scalar", lambda e, raw=raw, parts=parts: e.activation(parts[:, 0], raw[:], ACT.Copy),
                        [loaded[f"{name}_{ex}"], *w_free[k]], a_split)
                t = put("gpsimd", lambda e, raw=raw, parts=parts: e.tensor_tensor(
                    parts[:, 1], raw[:], parts[:, 0].bitcast(F32), ALU.subtract), [t], pool_split)
                raw_free[name] = [t]
                w_ready[name, ex] = t

        pick_zero = const(lambda e: e.memset(pick[:], 0.0), *early_free)
        const(lambda e: e.tensor_copy(vals[:, :, :, 0], tok_tile[:].unsqueeze(2).broadcast_to([P, NT, E])), iota_ok)
        const(lambda e: e.tensor_copy(vals[:, :, :, 1], tok_part[:, 0:1].unsqueeze(2).broadcast_to([P, NT, E])), iota_ok)
        t = const(lambda e: e.tensor_copy(vals[:, :, :, 2], probs[:]), probs_ready[vb])
        t = const(lambda e: e.tensor_tensor(rest[:], probs[:], vals[:, :, :, 2], ALU.subtract), t)
        t = const(lambda e: e.tensor_copy(vals[:, :, :, 3], rest[:]), t)
        vals_ready = const(lambda e: e.tensor_tensor(vals[:, :, :, 4], rest[:], vals[:, :, :, 3], ALU.subtract), t)

        load_expert(0)
        split_expert(0)
        load_expert(1)

        for hf in range(NH):
            n = MISC[hf]
            t = pe(lambda e, hf=hf, n=n: e.transpose(
                banks[n][:, 0:P], probs[:, hf * JT:(hf + 1) * JT, :].rearrange("p t e -> p (t e)"), ident[:]),
                probs_ready[vb], *released[n])
            t = vec_op(lambda e, hf=hf, n=n: e.tensor_copy(pt[:, hf * P:(hf + 1) * P], banks[n][:, 0:P]), t)
            released[n] = [t]
        pt_ready = t
        cur_i, cand_i = cur[:, 0:1], cur[:, 1:2]
        vec_op(lambda e: e.memset(cur_i, 0))
        cand_ready = vec_op(lambda e: e.memset(cand_i, 1 << FIRST_BIT))
        TOTAL = RHO[0]
        tot_ps = banks[TOTAL]
        for bit in range(FIRST_BIT, -1, -1):
            t = vec_op(lambda e: e.tensor_scalar(gt[:], pt[:], cand_i.bitcast(F32), None, ALU.is_ge, ALU.add,
                                                 accum_out=cnt[:, 0:1]), cand_ready, pt_ready)
            t = pe(lambda e: e.matmul(tot_ps[:, 0:1], same_expert[:], cnt[:, 0:1], start=True, stop=True),
                   t, router_consts, *released[TOTAL])
            fill()
            t = vec_op(lambda e, bit=bit: e.tensor_scalar(okbit[:, 0:1], tot_ps[:, 0:1], float(CAP), float(1 << bit),
                                                          ALU.is_ge, ALU.mult), t)
            released[TOTAL] = [t]
            if bit:
                cand_ready = vec_op(lambda e, bit=bit: e.scalar_tensor_tensor(
                    out=cand_i, in0=okbit[:, 0:1], scalar=1 << (bit - 1), in1=cur_i, op0=ALU.bitwise_or,
                    op1=ALU.bitwise_or), t)
            cur_ready = vec_op(lambda e: e.tensor_tensor(cur_i, okbit[:, 0:1], cur_i, ALU.bitwise_or), t, cand_ready)

        thr = cur_i.bitcast(F32)
        t_above = vec_op(lambda e: e.tensor_scalar(gt[:], pt[:], thr, None, ALU.is_gt, ALU.add,
                                                   accum_out=cnt[:, 0:1]), cur_ready)
        t = pe(lambda e: e.matmul(tot_ps[:, 0:1], same_expert[:], cnt[:, 0:1], start=True, stop=True), t_above,
               *released[TOTAL])
        fill()
        t_eq = vec_op(lambda e: e.tensor_scalar(eq[:], pt[:], thr, None, ALU.is_equal), t_above)
        left = vec_op(lambda e: e.tensor_scalar(cnt[:, 1:2], tot_ps[:, 0:1], -1.0, float(CAP), ALU.mult, ALU.add), t)
        released[TOTAL] = [left]

        def ranks(src, ready):
            for hf in range(NH):
                part = slice(hf * P, (hf + 1) * P)
                t = vec_op(lambda e, part=part: e.tensor_tensor_scan(scan[:, part], src[:, part], src[:, part], 0.0,
                                                                     ALU.add, ALU.bypass), ready)
            t = vec_op(lambda e: e.tensor_copy(cnt[:, 2:2 + NH], scan[:].rearrange("p (h k) -> p h k", h=NH)[:, :, P - 1]), t)

            def mm(e):
                e.matmul(tot_ps[:, 0:1], earlier_tile[:], cnt[:, 2:3], start=True, stop=True)
                e.matmul(tot_ps[:, 1:2], same_expert[:], cnt[:, 2:3], start=True, stop=False)
                return e.matmul(tot_ps[:, 1:2], earlier_tile[:], cnt[:, 3:4], start=False, stop=True)
            t = pe(mm, t, earlier_ok, *released[TOTAL])
            fill()
            t = vec_op(lambda e: e.tensor_copy(off[:], tot_ps[:, 0:NH]), t)
            released[TOTAL] = [t]
            return t

        t = ranks(eq, t_eq)
        for hf in range(NH):
            part = slice(hf * P, (hf + 1) * P)
            t2 = vec_op(lambda e, part=part, hf=hf: e.tensor_scalar(scan[:, part], scan[:, part], off[:, hf:hf + 1],
                                                                    cnt[:, 1:2], ALU.add, ALU.is_le), t, left)
        t = vec_op(lambda e: e.tensor_tensor(eq[:], eq[:], scan[:], ALU.mult), t2)
        chosen = vec_op(lambda e: e.tensor_tensor(gt[:], gt[:], eq[:], ALU.add), t)
        t = ranks(gt, chosen)
        for hf in range(NH):
            part = slice(hf * P, (hf + 1) * P)
            t2 = vec_op(lambda e, part=part, hf=hf: e.scalar_tensor_tensor(
                out=scan[:, part], in0=scan[:, part], scalar=off[:, hf:hf + 1], in1=gt[:, part], op0=ALU.add,
                op1=ALU.mult), t)
        n = MISC[0]
        t = pe(lambda e: [e.transpose(banks[n][:, hf * P:(hf + 1) * P], scan[:, hf * P:(hf + 1) * P], ident[:])
                          for hf in range(NH)][-1], t2, *released[n])
        fill()
        t = vec_op(lambda e: e.tensor_scalar(slot_i[:], banks[n][:, 0:NT * E], -1.0, None, ALU.add), t, *early_free)
        released[n] = [t]
        t3 = vec_op(lambda e: e.tensor_scalar(eq[:].bitcast(I32), slot_i[:], P - 1, None, ALU.bitwise_and), t)
        t4 = vec_op(lambda e: e.tensor_scalar(gt[:].bitcast(I32), slot_i[:], P.bit_length() - 1, None,
                                              ALU.arith_shift_right), t)
        vec_op(lambda e: e.tensor_copy(slot_c[:].rearrange("p t e -> p (t e)"), eq[:].bitcast(I32)), t3)
        slots_ready = vec_op(lambda e: e.tensor_copy(slot_a[:].rearrange("p t e -> p (t e)"), gt[:].bitcast(I32)), t4)

        pick_free, onehot_free, picked_free = [], [], []
        idx_free, score_free = {n: [] for n in range(NL)}, {n: [] for n in range(NL)}
        marked, listed, score_ready, gathers, scatters = {}, {}, {}, {}, {}
        xg_free = {k: [(stored[v], 16) for v in (2, 3)] for k in range(2)}

        def mark(ex):
            t = vec_op(lambda e: e.tensor_tensor(in_tile[:], slot_a[:, :, ex:ex + 1].broadcast_to([P, NT, A]),
                                                 iota_a[:].unsqueeze(1).broadcast_to([P, NT, A]), ALU.is_equal),
                       slots_ready, iota_ok)
            marked[ex] = vec_op(lambda e: e.tensor_tensor(
                pick[:, :, 0:V * A].rearrange("p t (v a) -> p t v a", v=V),
                in_tile[:].unsqueeze(2).broadcast_to([P, NT, V, A]),
                vals[:, :, ex, :].unsqueeze(3).broadcast_to([P, NT, V, A]), ALU.mult), t, vals_ready, *pick_free)

        def mark_slots(ex, q):
            tiles = slice(q * NT // 4, (q + 1) * NT // 4)
            marked[ex] = vec_op(lambda e: e.tensor_tensor(
                onehot[:, tiles, :], slot_c[:, tiles, ex:ex + 1].broadcast_to([P, NT // 4, P]),
                iota_slot_h[:].unsqueeze(1).broadcast_to([P, NT // 4, P]), ALU.is_equal), slots_ready, *onehot_free)
            return marked[ex]

        LIST, SLOTS = MISC

        def sum_list(ex, quarters=(None,)):
            for q in quarters:
                tiles = range(NT) if q is None else range(q * NT // 4, (q + 1) * NT // 4)
                ready = marked[ex] if q is None else mark_slots(ex, q)

                def mm(e, tiles=tiles):
                    for tile in tiles:
                        g = tile % G
                        ins = e.matmul(banks[LIST][32 * g:32 * g + 32, 0:P], pick[:, tile, :], onehot[:, tile, :],
                                       start=tile < G, stop=tile >= NT - G)
                    return ins
                t = pe(mm, ready, *released[LIST])
            pick_free[:], onehot_free[:] = [t], [t]
            t = vec_op(lambda e: e.tensor_copy(picked[:], banks[LIST][:, 0:P]), t, *picked_free)
            released[LIST] = [t]
            listed[ex] = t

        def fold_list(ex):
            k = ex % NL
            t = pe(lambda e: e.matmul(banks[SLOTS][:, 0:V * A], picked[:], fold[:, 0:V * A], start=True, stop=True),
                   listed[ex], *released[SLOTS])
            picked_free[:] = [t]
            t = vec_op(lambda e: e.tensor_copy(found[:], banks[SLOTS][:, 0:V * A].rearrange("p (v a) -> p v a", v=V)), t)
            released[SLOTS] = [t]
            t2 = vec_op(lambda e: e.scalar_tensor_tensor(out=idx[:, k, :], in0=found[:, 0, :], scalar=float(P),
                                                         in1=found[:, 1, :], op0=ALU.mult, op1=ALU.add), t, *idx_free[k])
            t3 = vec_op(lambda e: e.tensor_tensor(found[:, 2, :], found[:, 2, :], found[:, 3, :], ALU.add), t)
            score_ready[ex] = vec_op(lambda e: e.tensor_tensor(score[:, k, :], found[:, 2, :], found[:, 4, :], ALU.add),
                                     t3, *score_free[k])
            listed[ex] = t2

        def gather(ex):
            k = ex % 2
            for a in range(A):
                where = bass.IndirectOffsetOnAxis(idx[:, ex % NL, a:a + 1].bitcast(U32), 0)
                t = put("gpsimd", lambda e, a=a, where=where: e.indirect_dma_start(
                    xg[:, k, a, :], None, xn2_dram[:, :], where),
                    [listed[ex], *xg_free[k], *[(s, 16) for s in xn2_stored]], gathered[k], 16)
            gathers[ex] = t

        xgs_free = {0: [], 1: []}
        xgs_ready = {}

        def turn_gathered(ex):
            k = ex % 2
            for c in range(C):
                n = MISC[c]

                def four(e, c=c, n=n):
                    for a in range(A):
                        ins = e.transpose(banks[n][:, a * P:(a + 1) * P], xg[:, k, a, c * P:(c + 1) * P], ident[:])
                    return ins
                t = pe(four, gathers[ex], *released[n])
                hi, lo = xg_s[:, k, 0, c, :], xg_s[:, k, 1, c, :]
                t1 = put("scalar", lambda e, n=n, hi=hi: e.activation(hi, banks[n][:], ACT.Copy),
                         [t, *xgs_free[k]], a_split)
                t2 = vec_op(lambda e, n=n, hi=hi, lo=lo: e.tensor_tensor(lo, banks[n][:], hi.bitcast(F32),
                                                                         ALU.subtract), t1)
                released[n] = [t2]
            xg_free[k] = [t]
            xgs_ready[ex] = t2

        SUM = {0: (4, 5), 1: (0, 1)}
        hid_free = {n: [] for n in range(HC)}
        y_free = {0: [], 1: []}
        hid_ready, sum_done = {}, {}
        out_rows = out.rearrange("b s d -> (b s) d")

        def expert_up(ex, m):
            k, bank, h = ex % 2, UP[m % 2], m % HC

            def mm(e):
                for c in range(C):
                    ins = split_matmul(e, banks[bank][:], lambda i: w1_s[k][:, i, c, m * P:(m + 1) * P],
                                       lambda i: xg_s[:, k, i, c, :], c == 0, c == C - 1)
                return ins
            t = pe(mm, xgs_ready[ex], w_ready["w1", ex], *released[bank])
            cb = col["b1"] + ex * M + m
            t2 = put("scalar", lambda e: e.activation(hid[:, h, :], banks[bank][:], ACT.Gelu_apprx_tanh,
                                                      bias=vec[:, cb:cb + 1]), [t, *hid_free[h]], a_gelu)
            released[bank] = [t2]
            t3 = put("scalar", lambda e: e.activation(hid_s[:, h, 0, :], hid[:, h, :], ACT.Copy), [t2], a_split)
            hid_ready[ex, m] = vec_op(lambda e: e.tensor_tensor(hid_s[:, h, 1, :], hid[:, h, :],
                                                                hid_s[:, h, 0, :].bitcast(F32), ALU.subtract), t3)
            if m == M - 1:
                xgs_free[k] = [t]

        def expert_down(ex, m):
            k, h = ex % 2, m % HC
            sums = SUM[k]

            def mm(e):
                for a in range(A):
                    dst = banks[sums[a // 2]][:, a % 2 * D:(a % 2 + 1) * D]
                    for n, (i, j) in enumerate(SPLIT_TERMS):
                        ins = e.matmul(dst, hid_s[:, h, i, a * P:(a + 1) * P], w2_s[k][:, j, m, :],
                                       start=(m == 0 and n == 0 and a % 2 == 0), stop=(m == M - 1 and n == 2),
                                       skip_group_check=True)
                return ins
            t = pe(mm, hid_ready[ex, m], w_ready["w2", ex], *released[sums[0]], *released[sums[1]])
            hid_free[h] = [t]
            sum_done[ex] = t

        def expert_out(ex):
            k = ex % 2
            w_free[k] = [sum_done[ex]]
            rows = []
            for a in range(A):
                bank = SUM[k][a // 2]
                t = vec_op(lambda e, a=a, bank=bank: e.tensor_tensor(
                    y[:, k, a, :], banks[bank][:, a % 2 * D:(a % 2 + 1) * D], b2_rep[:, ex, :], ALU.add),
                    sum_done[ex], b2_loaded, *y_free[k])
                released[bank] = [t]
                rows.append(vec_op(lambda e, a=a: e.tensor_scalar(y[:, k, a, :], y[:, k, a, :], score[:, ex % NL, a:a + 1],
                                                                  None, ALU.mult), t, score_ready[ex]))
            score_free[ex % NL] = [rows[-1]]
            before = [scatters[ex - 1]] if ex else [(s, 16) for s in stored]
            for a in range(A):
                where = bass.IndirectOffsetOnAxis(idx[:, ex % NL, a:a + 1].bitcast(U32), 0)
                t = put("gpsimd", lambda e, a=a, where=where: e.indirect_dma_start(
                    out_rows, where, y[:, k, a, :], None, compute_op=ALU.add), [rows[a], *before], scattered, 16)
            scatters[ex] = t
            y_free[k] = [t]
            idx_free[ex % NL] = [t]

        for ex in range(2):
            mark(ex)
            fill(LIST_FILL[ex])
            sum_list(ex, range(4))
            fold_list(ex)
            gather(ex)
        b2_loaded = load("b2", b2_rep[:], b2.rearrange("e d -> (e d)").partition_broadcast(P),
                         [(stored[v], 16) for v in (4, 5)])
        for k in range(2):
            xgs_free[k] = [*tr_free[0], *tr_free[1]]
        turn_gathered(0)
        fill(len(filler) + 1)
        for h in range(HC):
            hid_free[h] = [*u_free[0], *u_free[1]]
        for k in range(2):
            y_free[k] = [*u_free[0], *u_free[1]]
        w_free[1] = [*tr_free[1], *u_free[1], (stored[va], 16), (stored[vb], 16)]

        LAG = 2
        for m in range(LAG):
            expert_up(0, m)
        split_expert(1)
        for ex in range(E):
            for m in range(M):
                ahead = m + LAG
                if ahead < M:
                    expert_up(ex, ahead)
                elif ex + 1 < E:
                    expert_up(ex + 1, ahead - M)
                expert_down(ex, m)
                if m == 0 and ex + 2 < E:
                    load_expert(ex + 2)
                    mark(ex + 2)
                if m < 4 and ex + 2 < E:
                    mark_slots(ex + 2, m)
                if m == 2 and ex + 1 < E:
                    turn_gathered(ex + 1)
                if m == 4 and ex + 2 < E:
                    sum_list(ex + 2)
                if m == 5 and ex + 2 < E:
                    fold_list(ex + 2)
                    gather(ex + 2)
            expert_out(ex)
            if ex + 2 < E:
                split_expert(ex + 2)
        put("gpsimd", lambda e: e.nop(), [scatters[E - 1]])

        block = ctx.enter_context(nc.Block())

        @block.sync
        def _(eng):
            plan.run("sync", eng)

        @block.gpsimd
        def _(eng):
            plan.run("gpsimd", eng)

        @block.scalar
        def _(eng):
            plan.run("scalar", eng)

        @block.tensor
        def _(eng):
            plan.run("tensor", eng)

        @block.vector
        def _(eng):
            plan.run("vector", eng)


_INS = ['x', 'ctx_1024', 'mask_BxS2_ik0', 'L0_xattn_Ws', 'L0_xattn_W', 'L0_xattn_w', 'L0_xattn_b', 'L0_xattn_Wcw',
        'L0_xattn_bcw', 'L0_xattn_Wcb', 'L0_xattn_bcb', 'L0_ffn_gate', 'L0_ffn_W1', 'L0_ffn_b1', 'L0_ffn_W2',
        'L0_ffn_b2', 'L0_ffn_Ws1', 'L0_ffn_bs1', 'L0_ffn_Ws2', 'L0_ffn_bs2']


def kernel(**inputs):
    import numpy as _np
    import concourse.bacc as _bacc
    from concourse import mybir as _mybir
    from concourse.bass_utils import run_bass_kernel_spmd as _run

    nc = _bacc.Bacc("TRN2", target_bir_lowering=False, num_devices=1)
    arrays, args = {}, []
    for name in _INS:
        a = _np.ascontiguousarray(inputs[name])
        arrays[f"in_{name}_dram"] = a
        args.append(nc.dram_tensor(f"in_{name}_dram", a.shape, _mybir.dt.from_np(a.dtype), kind="ExternalInput").ap())
    shape = tuple(inputs['x'].shape)
    out = nc.dram_tensor("out_0_dram", shape, _mybir.dt.float32, kind="ExternalOutput").ap()
    xn2 = nc.dram_tensor("xn2_dram", (shape[0] * shape[1], shape[2]), _mybir.dt.float32, kind="Internal").ap()
    xattn_moe_kernel(nc, *args, out, xn2)
    r = _run(nc, [arrays], core_ids=[0])
    return r.results[0]["out_0_dram"]
```
